# Optimizing a Trainium2 kernel written in Bass

```python
import numpy as np
import jax
import jax.numpy as jnp

def _softmax(x, axis=-1):
    return jax.nn.softmax(x, axis=axis)

def _gelu(x):
    return jax.nn.gelu(x, approximate=True)

def _silu(x):
    return jax.nn.silu(x)

def _sigmoid(x):
    return jax.nn.sigmoid(x)

def _layernorm(x, axis=-1, eps=1e-05):
    m = jnp.mean(x, axis=axis, keepdims=True)
    v = jnp.var(x, axis=axis, keepdims=True)
    return (x - m) / jnp.sqrt(v + eps)

def _scatter_add(tgt, idx, src, axis=0):
    return tgt.at[idx].add(src)

def _segment_sum(src, seg, n):
    return jax.ops.segment_sum(src, seg, n)
kernel_name = 'mk_pixart_seq_d1_seqx_r8_355142'

def setup_inputs(seed: int=0):
    np.random.seed(seed)
    _w = jnp.asarray

    def _rec_inputs():
        import jax
        import jax.numpy as jnp
        _rk = jax.random.key(seed)
        x = -0.0002928 + 1 * jax.random.normal(jax.random.fold_in(_rk, 1), (32, 128, 128), jnp.float32)
        _lenS = 128 - jax.random.randint(jax.random.fold_in(_rk, 7), (32,), 0, max(1, 128 // 4) + 1, jnp.int32)
        _lenS2 = 77 - jax.random.randint(jax.random.fold_in(_rk, 8), (32,), 0, max(1, 77 // 4) + 1, jnp.int32)
        cond_1024 = 0.0061147 + 1.02565 * jax.random.normal(jax.random.fold_in(_rk, 11), (32, 128), jnp.float32)
        _ctx_1024P = jax.random.normal(jax.random.fold_in(_rk, 12), (32, 16, 128), jnp.float32)
        _ctx_1024c = jax.random.dirichlet(jax.random.fold_in(_rk, 512), 0.3 * jnp.ones((16,), jnp.float32), (32, 77))
        _ctx_1024t = jnp.einsum('bsk,bkd->bsd', _ctx_1024c, _ctx_1024P)
        _ctx_1024t = _ctx_1024t * jax.lax.rsqrt(jnp.mean(jnp.square(_ctx_1024t)) + 1e-12) * 0.953939
        ctx_1024 = -0.00265004 + 0.998804 * (_ctx_1024t + 0.3 * jax.random.normal(jax.random.fold_in(_rk, 612), (32, 77, 128), jnp.float32))
        return (x, cond_1024, ctx_1024)
    x, cond_1024, ctx_1024 = _rec_inputs()

    def _L0_xcond_setup():
        import jax, jax.numpy as jnp
        import numpy as np
        LN_EPS = 1e-06

        def _ln(x):
            mu = jnp.mean(x, axis=-1, keepdims=True)
            var = jnp.var(x, axis=-1, keepdims=True)
            return (x - mu) * jax.lax.rsqrt(var + LN_EPS)
        key = jax.random.key(seed)
        H, NH = (128, 16)
        B, N, S = (4, 128, 77)
        MLP = int(H * 4.0)
        ks = jax.random.split(key, 20)
        s = 1.0 / np.sqrt(H)
        return {'x': jax.random.normal(ks[0], (B, N, H), jnp.float32), 'c': jax.random.normal(ks[1], (B, H), jnp.float32), 'context': jax.random.normal(ks[2], (B, S, H), jnp.float32), 'W_mod': jax.random.normal(ks[3], (H, 6 * H), jnp.float32) * s, 'b_mod': jnp.zeros((6 * H,), jnp.float32), 'W_qkv': jax.random.normal(ks[4], (H, 3 * H), jnp.float32) * s, 'b_qkv': jnp.zeros((3 * H,), jnp.float32), 'W_proj': jax.random.normal(ks[5], (H, H), jnp.float32) * s, 'b_proj': jnp.zeros((H,), jnp.float32), 'W_qc': jax.random.normal(ks[6], (H, H), jnp.float32) * s, 'b_qc': jnp.zeros((H,), jnp.float32), 'W_kvc': jax.random.normal(ks[7], (H, 2 * H), jnp.float32) * s, 'b_kvc': jnp.zeros((2 * H,), jnp.float32), 'W_cproj': jax.random.normal(ks[8], (H, H), jnp.float32) * s, 'b_cproj': jnp.zeros((H,), jnp.float32), 'W_mlp1': jax.random.normal(ks[9], (H, MLP), jnp.float32) * s, 'b_mlp1': jnp.zeros((MLP,), jnp.float32), 'W_mlp2': jax.random.normal(ks[10], (MLP, H), jnp.float32) * (1.0 / np.sqrt(MLP)), 'b_mlp2': jnp.zeros((H,), jnp.float32)}
    _L0_xcond_all = _L0_xcond_setup()
    _L0_xcond_in = {k: v for k, v in _L0_xcond_all.items() if k in ('W_mod', 'b_mod', 'W_qkv', 'b_qkv', 'W_proj', 'b_proj', 'W_qc', 'b_qc', 'W_kvc', 'b_kvc', 'W_cproj', 'b_cproj', 'W_mlp1', 'b_mlp1', 'W_mlp2', 'b_mlp2')}
    del _L0_xcond_all
    return {'x': x, 'cond_1024': cond_1024, 'ctx_1024': ctx_1024, 'L0_xcond_W_mod': _L0_xcond_in['W_mod'], 'L0_xcond_b_mod': _L0_xcond_in['b_mod'], 'L0_xcond_W_qkv': _L0_xcond_in['W_qkv'], 'L0_xcond_b_qkv': _L0_xcond_in['b_qkv'], 'L0_xcond_W_proj': _L0_xcond_in['W_proj'], 'L0_xcond_b_proj': _L0_xcond_in['b_proj'], 'L0_xcond_W_qc': _L0_xcond_in['W_qc'], 'L0_xcond_b_qc': _L0_xcond_in['b_qc'], 'L0_xcond_W_kvc': _L0_xcond_in['W_kvc'], 'L0_xcond_b_kvc': _L0_xcond_in['b_kvc'], 'L0_xcond_W_cproj': _L0_xcond_in['W_cproj'], 'L0_xcond_b_cproj': _L0_xcond_in['b_cproj'], 'L0_xcond_W_mlp1': _L0_xcond_in['W_mlp1'], 'L0_xcond_b_mlp1': _L0_xcond_in['b_mlp1'], 'L0_xcond_W_mlp2': _L0_xcond_in['W_mlp2'], 'L0_xcond_b_mlp2': _L0_xcond_in['b_mlp2']}

def reference(x, cond_1024, ctx_1024, L0_xcond_W_mod, L0_xcond_b_mod, L0_xcond_W_qkv, L0_xcond_b_qkv, L0_xcond_W_proj, L0_xcond_b_proj, L0_xcond_W_qc, L0_xcond_b_qc, L0_xcond_W_kvc, L0_xcond_b_kvc, L0_xcond_W_cproj, L0_xcond_b_cproj, L0_xcond_W_mlp1, L0_xcond_b_mlp1, L0_xcond_W_mlp2, L0_xcond_b_mlp2):
    import jax
    import jax.numpy as jnp

    def _L0_xcond_ref(x, c, context, W_mod, b_mod, W_qkv, b_qkv, W_proj, b_proj, W_qc, b_qc, W_kvc, b_kvc, W_cproj, b_cproj, W_mlp1, b_mlp1, W_mlp2, b_mlp2):
        import jax, jax.numpy as jnp
        import numpy as np
        LN_EPS = 1e-06

        def _ln(x):
            mu = jnp.mean(x, axis=-1, keepdims=True)
            var = jnp.var(x, axis=-1, keepdims=True)
            return (x - mu) * jax.lax.rsqrt(var + LN_EPS)
        B, N, H = x.shape
        NH = 16
        hd = H // NH
        scale = hd ** (-0.5)
        c_proj = jax.nn.silu(c) @ W_mod + b_mod
        shift_a, scale_a, gate_a, shift_m, scale_m, gate_m = jnp.split(c_proj, 6, axis=-1)

        def modulate(t, shift, sc):
            return t * (1 + sc[:, None]) + shift[:, None]
        x_norm = modulate(_ln(x), shift_a, scale_a)
        qkv = x_norm @ W_qkv + b_qkv
        q, k, v = jnp.split(qkv, 3, axis=-1)
        q = q.reshape(B, N, NH, hd).transpose(0, 2, 1, 3)
        k = k.reshape(B, N, NH, hd).transpose(0, 2, 1, 3)
        v = v.reshape(B, N, NH, hd).transpose(0, 2, 1, 3)
        attn_w = jax.nn.softmax(jnp.einsum('bhqd,bhkd->bhqk', q, k) * scale, axis=-1)
        attn_out = jnp.einsum('bhqk,bhkd->bhqd', attn_w, v)
        attn_out = attn_out.transpose(0, 2, 1, 3).reshape(B, N, H)
        attn_out = attn_out @ W_proj + b_proj
        x = x + gate_a[:, None] * attn_out
        S = context.shape[1]
        q_c = _ln(x) @ W_qc + b_qc
        kv_c = _ln(context) @ W_kvc + b_kvc
        k_c, v_c = jnp.split(kv_c, 2, axis=-1)
        q_c = q_c.reshape(B, N, NH, hd).transpose(0, 2, 1, 3)
        k_c = k_c.reshape(B, S, NH, hd).transpose(0, 2, 1, 3)
        v_c = v_c.reshape(B, S, NH, hd).transpose(0, 2, 1, 3)
        c_attn_w = jax.nn.softmax(jnp.einsum('bhqd,bhsd->bhqs', q_c, k_c) * scale, axis=-1)
        c_attn_out = jnp.einsum('bhqs,bhsd->bhqd', c_attn_w, v_c)
        c_attn_out = c_attn_out.transpose(0, 2, 1, 3).reshape(B, N, H)
        c_attn_out = c_attn_out @ W_cproj + b_cproj
        x = x + c_attn_out
        x_norm2 = modulate(_ln(x), shift_m, scale_m)
        h = jax.nn.gelu(x_norm2 @ W_mlp1 + b_mlp1)
        h = h @ W_mlp2 + b_mlp2
        x = x + gate_m[:, None] * h
        return x
    x = _L0_xcond_ref(x, cond_1024, ctx_1024, L0_xcond_W_mod, L0_xcond_b_mod, L0_xcond_W_qkv, L0_xcond_b_qkv, L0_xcond_W_proj, L0_xcond_b_proj, L0_xcond_W_qc, L0_xcond_b_qc, L0_xcond_W_kvc, L0_xcond_b_kvc, L0_xcond_W_cproj, L0_xcond_b_cproj, L0_xcond_W_mlp1, L0_xcond_b_mlp1, L0_xcond_W_mlp2, L0_xcond_b_mlp2)
    return x

_drawn_inputs = setup_inputs


def setup_inputs(seed=0):
    import zlib

    import numpy as np

    out = dict(_drawn_inputs(seed))
    spreads = {'L0_xcond_b_mod': (0.0, 0.1),
     'L0_xcond_b_qkv': (0.0, 0.1),
     'L0_xcond_b_proj': (0.0, 0.1),
     'L0_xcond_b_qc': (0.0, 0.493),
     'L0_xcond_b_kvc': (0.0, 0.1),
     'L0_xcond_b_cproj': (0.0, 0.1),
     'L0_xcond_b_mlp1': (0.0, 0.1),
     'L0_xcond_b_mlp2': (0.0, 0.1)}
    factors = {}
    for name, (base, spread) in spreads.items():
        noise = np.random.default_rng([zlib.crc32(name.encode()), seed]).standard_normal(out[name].shape)
        drawn = base * np.exp(spread * noise) if base else spread * noise
        out[name] = jnp.asarray(drawn.astype(out[name].dtype))
    for name, factor in factors.items():
        out[name] = (out[name] * factor).astype(out[name].dtype)
    return out
```

```python
from contextlib import ExitStack

import concourse.bass as bass
from concourse import mybir

B, T, C = 32, 128, 128
H, D = 16, 8
S = 77
F = 512
G = 2
NPAIR = B // G
GT, GS = G * T, G * S
NF = F // 128
MG = 4
NGRP = B // MG
NU = 8
EPS = 1e-6
SCALE = float(D) ** -0.5
COMBOS = [(0, 0), (0, 1), (0, 2), (1, 0), (1, 1), (2, 0)]
NCMB = len(COMBOS)
KMAX = 96
MROW = 96

MISC = [("proj", "back1", 0), ("max_c1", "back2", 1), ("y_t", "back1", 0), ("ctx_t", "back1", 1),
        ("kv_c", "back1", 0), ("x1_t", "back1", 1), ("max_s0", "here", 0), ("q_c", "back1", 1),
        ("x_t", "ahead", 0), ("qk", "ahead", 1), ("max_s1", "here", 0), ("proj_c", "back2", 1),
        ("v", "ahead", 0), ("yc_t", "back2", 1), ("max_c0", "back1", 0)]
BANK = {name: bank for name, _, bank in MISC}


class Pair:

    def __init__(self, i, k):
        self.i, self.k = i, k
        self.n = 2 * i + k
        self.par = k % 2
        self.turn = i + k // 2

    def exists(self):
        return not isinstance(self.n, int) or 0 <= self.n < NPAIR

    def first(self, m=1):
        return isinstance(self.n, int) and self.n < m

    def shift(self, d):
        return Pair(self.i, self.k + d)


class Slot:
    def __init__(self, i, k):
        here = Pair(i, k)
        self.pairs = {"ahead": here.shift(1), "here": here, "back1": here.shift(-1), "back2": here.shift(-2)}
        self.ahead, self.here, self.back1, self.back2 = (
            p if p.exists() else None for p in self.pairs.values())
        self.i, self.k = i, k

    def before(self):
        return Slot(self.i, self.k - 1)

    def job_before(self, name):
        names = [m[0] for m in MISC]
        slot, at = self, names.index(name)
        for _ in range(3 * len(MISC)):
            at -= 1
            if at < 0:
                slot, at = slot.before(), len(MISC) - 1
            job, whose, bank = MISC[at]
            if bank == BANK[name] and slot.pairs[whose].exists():
                return job, slot.pairs[whose]
        return None


FIRST_SLOT, LAST_SLOT = -1, NPAIR + 1
LOOP = (2, (NPAIR - 2) // 2)


def slots(engine, emit):
    for s in range(FIRST_SLOT, 2 * LOOP[0]):
        emit(Slot(s // 2, s % 2))
    with engine.Fori(LOOP[0], LOOP[1]) as i:
        emit(Slot(i, 0))
        emit(Slot(i, 1))
    for s in range(2 * LOOP[1], LAST_SLOT + 1):
        emit(Slot(s // 2, s % 2))


def block_kernel(nc, x, cond, ctx, w_mod, b_mod, w_qkv, b_qkv, w_proj, b_proj, w_qc, b_qc, w_kvc, b_kvc,
                 w_cproj, b_cproj, w_mlp1, b_mlp1, w_mlp2, b_mlp2, out):
    f32, bf16 = mybir.dt.float32, mybir.dt.bfloat16
    ALU, ACT, AX = mybir.AluOpType, mybir.ActivationFunctionType, mybir.AxisListType

    es = ExitStack()
    with es:
        def sb(name, shape, dt=f32):
            return es.enter_context(nc.sbuf_tensor(name, shape, dt))

        def pairbuf(name, shape, dt=f32):
            return [sb(f"{name}{i}", shape, dt) for i in range(2)]

        sems = {}

        def sem(name):
            sems[name] = es.enter_context(nc.semaphore(name))
            return sems[name]

        xs = sb("xs", [T, B, C])
        ctx_sb = sb("ctx_sb", [S, B, C])
        cond_sb = sb("cond_sb", [B, C])
        wmod_sb = sb("wmod_sb", [C, 6 * C])
        wqkv_sb = sb("wqkv_sb", [C, 3 * C])
        wproj_sb = sb("wproj_sb", [C, C])
        wqc_sb = sb("wqc_sb", [C, C])
        wkvc_sb = sb("wkvc_sb", [C, 2 * C])
        wcproj_sb = sb("wcproj_sb", [C, C])
        w1_sb = sb("w1_sb", [C, F])
        w2_sb = sb("w2_sb", [128, NF, C])
        wdh = sb("wdh", [C, 4, C])
        bmod_sb = sb("bmod_sb", [C, 6])
        bdh = sb("bdh", [C, 4])
        bv_sb = sb("bv_sb", [C, 2])
        bo_sb = sb("bo_sb", [C, 3])
        b1_sb = sb("b1_sb", [128, NF])
        bo2 = sb("bo2", [C, 2])
        ident = sb("ident", [128, 128])
        ident16 = sb("ident16", [128, 128], bf16)
        ones_m = sb("ones_m", [128, 4, 32])
        condT = sb("condT", [C, B])
        tanh_c = sb("tanh_c", [C, B])
        siluT = sb("siluT", [C, B])
        mod = sb("mod", [C, 6, B])
        gb_a = sb("gb_a", [C, B])
        gb_m = sb("gb_m", [C, B])
        eps_sb = sb("eps_sb", [128, MG])
        mhalf = sb("mhalf", [128, MG])

        q_st = pairbuf("q_st", [128, H, GT], bf16)
        k_st = pairbuf("k_st", [128, H, GT], bf16)
        qc_st = pairbuf("qc_st", [128, H, GT], bf16)
        kc_st = pairbuf("kc_st", [128, H, GS], bf16)
        v_m = pairbuf("v_m", [T, G, H, 32])
        vc_m = pairbuf("vc_m", [S, G, H, 32])
        ln = {}
        for kind, rows in (("x", T), ("ctx", S), ("x1", T)):
            ln[kind] = dict(rows=rows, stats=sb(f"{kind}_stats", [rows, G, 6]), mv=sb(f"{kind}_mv", [rows, G, 2]),
                            ve=sb(f"{kind}_ve", [rows, G]), rstd=sb(f"{kind}_rstd", [rows, G]),
                            xn=sb(f"{kind}_n", [rows, G, C]))
        xmT = sb("xmT", [C, GT])
        cT = sb("cT", [C, GS])
        x1T = sb("x1T", [C, GT])
        qp = sb("qp", [C, 3, GT], bf16)
        kp = sb("kp", [C, 3, GT], bf16)
        qcp = sb("qcp", [C, 3, GT], bf16)
        kcp = sb("kcp", [C, 3, GS], bf16)
        qr = sb("qr", [C, GT])
        kr = sb("kr", [C, GT])
        qcr = sb("qcr", [C, GT])
        kcr = sb("kcr", [C, GS])
        mx = sb("mx", [T, G, H])
        mxc = sb("mxc", [T, G, H])
        nm = sb("nm", [T, G, 2, H], bf16)
        nmc = sb("nmc", [T, G, 2, H], bf16)
        nmT = sb("nmT", [2 * H, G, T], bf16)
        nmcT = sb("nmcT", [2 * H, G, T], bf16)
        p_s = [sb(f"p_s{i}", [T, 4, T]) for i in range(2)]
        p_c = [sb(f"p_c{i}", [S, 4, T]) for i in range(2)]
        rden = sb("rden", [C, GT])
        rdenc = sb("rdenc", [C, GT])
        oT = sb("oT", [C, GT])
        ocT = sb("ocT", [C, GT])
        yT = sb("yT", [C, GT])
        ycT = sb("ycT", [C, GT])

        m_stats = sb("m_stats", [T, MG, 6])
        m_mv = sb("m_mv", [T, MG, 2])
        m_ve = sb("m_ve", [T, MG])
        m_rstd = sb("m_rstd", [T, MG])
        m_n = pairbuf("m_n", [T, MG, C])
        m_nT = pairbuf("m_nT", [C, MG * T])
        hT = pairbuf("hT", [128, NF, MG * T])
        m_y = pairbuf("m_y", [C, MG * T])
        m_out = pairbuf("m_out", [T, MG, C])

        ps = [es.enter_context(nc.psum_tensor(f"ps{i}", [128, 512], f32)) for i in range(8)]
        ps_max, ps_st, ps_o, ps_d, ps_misc = ps[0:2], ps[2:4], ps[4], ps[5], ps[6:8]

        for name in ("w_in b_in x_in0 x_in1 x_in2 x_in3 c_in0 c_in1 c_in2 c_in3 z_set z_pool id_set wdh_set cond_t condT_set "
                     "tanh_set sig_set silu_set mod_ps mod_set mod_1 bo_ps bo_set gb_set "
                     "xt_ps qk_ps v_ps ctxt_ps kvc_ps proj_ps yt_ps x1t_ps qc_ps projc_ps yct_ps mts_ps mtc_ps "
                     "smax_ps smaxc_ps st_ps stc_ps pv_ps pvc_ps "
                     "xmT_set qk0_set v_set cT_set kvc0_set y_set x1T_set qc0_set yc_set exp_set expc_set "
                     "qkr_set kcr_set qcr_set mx_set mxc_set nmh_set nm_set nmch_set nmc_set nmT_set nmcT_set "
                     "rden_set oT_set rdenc_set ocT_set x1_set x2_set "
                     "q1_set q2_set k2_set kc1_set kc2_set qc1_set qc2_set "
                     "q_in0 q_in1 k_in0 k_in1 qc_in0 qc_in1 kc_in0 kc_in1 m_in0 m_in1 mc_in0 mc_in1 "
                     "m_stats_set m_mv_set m_ve_set m_rstd_set m_n_set m_nt_ps m_nT_set m_h_ps m_hT_set m_y_ps "
                     "m_y_set m_yt_ps m_out_set out0 out1").split():
            sem(name)
        for name in ("SP", "Pool", "DVE"):
            sem(f"held_{name}")
        for kind in ln:
            for what in ("stats", "mv", "ve", "rstd", "n"):
                sem(f"{kind}_{what}_set")

        def w(eng, name, value):
            eng.wait_ge(sems[name], value)

        def hold(eng, name, value):
            eng.wait_ge(sems[name], value)
            eng.sem_inc(sems[f"held_{eng.engine.name}"], 1)

        EMPTIED = {"proj": ("y_set", lambda p: p.n + 1), "max_c1": ("nmcT_set", lambda p: 2 * p.n + 2),
                   "y_t": ("x1_set", lambda p: p.n + 1), "ctx_t": ("cT_set", lambda p: p.n + 1),
                   "kv_c": ("kcr_set", lambda p: p.n + 1), "x1_t": ("x1T_set", lambda p: p.n + 1),
                   "max_s0": ("nmT_set", lambda p: 2 * p.n + 1), "q_c": ("qcr_set", lambda p: p.n + 1),
                   "x_t": ("xmT_set", lambda p: p.n + 1), "qk": ("qkr_set", lambda p: p.n + 1),
                   "max_s1": ("nmT_set", lambda p: 2 * p.n + 2), "proj_c": ("yc_set", lambda p: p.n + 1),
                   "v": ("v_set", lambda p: p.n + 1), "yc_t": ("x2_set", lambda p: p.n + 1),
                   "max_c0": ("nmcT_set", lambda p: 2 * p.n + 1)}

        def batch(p, b):
            return bass.ds(2 * p.n + b, 1) if not isinstance(p.n, int) else slice(2 * p.n + b, 2 * p.n + b + 1)

        def batches(p):
            return bass.ds(2 * p.n, G) if not isinstance(p.n, int) else slice(2 * p.n, 2 * p.n + G)

        def column(tile, p, b):
            return tile[:, batch(p, b)]

        block = es.enter_context(nc.Block())

        @block.sync
        def _(sp):
            NW = 9
            sp.dma_start(cond_sb[:], cond).then_inc(sems["w_in"], 16)
            sp.dma_start(wmod_sb[:], w_mod).then_inc(sems["w_in"], 16)
            q4 = B // 4
            sp.dma_start(xs[:, 0:q4], x[0:q4].rearrange("b t c -> t b c")).then_inc(sems["x_in0"], 16)
            sp.dma_start(wqkv_sb[:], w_qkv).then_inc(sems["w_in"], 16)
            with nc.allow_non_contiguous_dma(reason="bias columns"):
                sp.dma_start(bmod_sb[:], b_mod.rearrange("(k c) -> c k", k=6)).then_inc(sems["b_in"], 16)
                for n, (src, at) in enumerate(((b_qkv, 0), (b_qkv, C), (b_qc, 0), (b_kvc, 0))):
                    for d in range(D):
                        sp.dma_start(bdh[d * H:(d + 1) * H, n:n + 1],
                                     src[at + d:at + C:D].rearrange("(h o) -> h o", o=1)).then_inc(sems["b_in"], 16)
                for n, (src, at) in enumerate(((b_qkv, 2 * C), (b_kvc, C))):
                    sp.dma_start(bv_sb[:, n:n + 1],
                                 src[at:at + C].rearrange("(c o) -> c o", o=1)).then_inc(sems["b_in"], 16)
                for n, src in enumerate((b_proj, b_cproj, b_mlp2)):
                    sp.dma_start(bo_sb[:, n:n + 1], src.rearrange("(c o) -> c o", o=1)).then_inc(sems["b_in"], 16)
                sp.dma_start(b1_sb[:], b_mlp1.rearrange("(k c) -> c k", k=NF)).then_inc(sems["b_in"], 16)
            for dst, src in ((wproj_sb, w_proj), (wqc_sb, w_qc), (wkvc_sb, w_kvc), (wcproj_sb, w_cproj), (w1_sb, w_mlp1)):
                sp.dma_start(dst[:], src).then_inc(sems["w_in"], 16)
            sp.dma_start(w2_sb[:], w_mlp2.rearrange("(k f) c -> f k c", k=NF)).then_inc(sems["w_in"], 16)
            sp.dma_start(ctx_sb[:, 0:q4], ctx[0:q4].rearrange("b t c -> t b c")).then_inc(sems["c_in0"], 16)
            for n in range(1, 4):
                sp.dma_start(xs[:, n * q4:(n + 1) * q4],
                             x[n * q4:(n + 1) * q4].rearrange("b t c -> t b c")).then_inc(sems[f"x_in{n}"], 16)
                sp.dma_start(ctx_sb[:, n * q4:(n + 1) * q4],
                             ctx[n * q4:(n + 1) * q4].rearrange("b t c -> t b c")).then_inc(sems[f"c_in{n}"], 16)

            def stack(dst, parts, which, name):
                for c, combo in enumerate(COMBOS):
                    sp.dma_start(dst[D * c:D * c + D], parts[:, combo[which]]).then_inc(sems[name], 16)

            def max_rows(dst, b, src, name):
                sp.dma_start(dst[MROW:MROW + 2, :, b * T:(b + 1) * T], src[:, b]).then_inc(sems[name], 16)

            def slot(s):
                if s.back2:
                    p = s.back2
                    w(sp, "nmcT_set", 2 * p.n + 2)
                    max_rows(qc_st[p.par], 1, nmcT, f"mc_in{p.par}")
                if s.back1:
                    p = s.back1
                    hold(sp, "kc2_set", p.n + 1)
                    if not p.first(2):
                        w(sp, "pvc_ps", NU * (p.n - 1))
                    stack(kc_st[p.par], kcp, 1, f"kc_in{p.par}")
                if s.here:
                    p = s.here
                    w(sp, "nmT_set", 2 * p.n + 1)
                    max_rows(q_st[p.par], 0, nmT, f"m_in{p.par}")
                if s.back1:
                    p = s.back1
                    w(sp, "qc2_set", p.n + 1)
                    stack(qc_st[p.par], qcp, 0, f"qc_in{p.par}")
                if s.here:
                    p = s.here
                    w(sp, "nmT_set", 2 * p.n + 2)
                    max_rows(q_st[p.par], 1, nmT, f"m_in{p.par}")
                if s.ahead:
                    p = s.ahead
                    hold(sp, "q2_set", p.n + 1)
                    if not p.first(2):
                        w(sp, "pv_ps", NU * (p.n - 1))
                    stack(q_st[p.par], qp, 0, f"q_in{p.par}")
                    w(sp, "k2_set", p.n + 1)
                    stack(k_st[p.par], kp, 1, f"k_in{p.par}")
                if s.back1:
                    p = s.back1
                    w(sp, "nmcT_set", 2 * p.n + 1)
                    max_rows(qc_st[p.par], 0, nmcT, f"mc_in{p.par}")

            w(sp, "z_set", 1)
            slots(sp, slot)

            def store(g, par):
                w(sp, "m_out_set", g + 1)
                src = m_out[par][:]
                at = bass.ds(g, 1) if not isinstance(g, int) else slice(g, g + 1)
                dst = out.rearrange("(g b) t c -> g t b c", b=MG)[at].rearrange("o t b c -> t (o b) c")
                sp.dma_start(dst, src).then_inc(sems[f"out{par}"], 16)

            with sp.Fori(0, NGRP // 2) as i:
                store(2 * i, 0)
                store(2 * i + 1, 1)
            w(sp, "out0", 16 * (NGRP // 2))
            w(sp, "out1", 16 * (NGRP // 2))

        @block.gpsimd
        def _(pool):
            nc.gpsimd.memset(ident[:], 0.0).then_inc(sems["z_pool"], 1)
            pool.wait_ge(sems["z_pool"], 1)
            nc.gpsimd.affine_select(out=ident[:], in_=ident[:], compare_op=ALU.not_equal, fill=1.0, base=0,
                                    pattern=[[-1, 128]], channel_multiplier=1).then_inc(sems["z_pool"], 1)
            pool.wait_ge(sems["z_pool"], 2)
            nc.gpsimd.tensor_copy(ident16[:], ident[:]).then_inc(sems["id_set"], 1)
            nc.gpsimd.memset(eps_sb[:], EPS).then_inc(sems["z_pool"], 1)
            nc.gpsimd.memset(mhalf[:], -0.5).then_inc(sems["z_pool"], 1)
            pool.wait_ge(sems["w_in"], 16 * 9)
            for n, (src, at) in enumerate(((wqkv_sb, 0), (wqkv_sb, C), (wqc_sb, 0), (wkvc_sb, 0))):
                nc.gpsimd.tensor_copy(wdh[:, n].rearrange("c (d h) -> c d h", d=D),
                                      src[:, at:at + C].rearrange("c (h d) -> c d h", d=D)).then_inc(sems["wdh_set"], 1)
            pool.wait_ge(sems["z_pool"], 4)

            def rstd(kind, p):
                L = ln[kind]
                w(pool, f"{kind}_mv_set", p.n + 1)
                nc.gpsimd.tensor_tensor(L["ve"][:], L["mv"][:, :, 1], eps_sb[0:L["rows"], 0:G],
                                        ALU.add).then_inc(sems[f"{kind}_ve_set"], 1)
                w(pool, f"{kind}_ve_set", p.n + 1)
                if not p.first():
                    w(pool, f"{kind}_n_set", p.n)
                nc.gpsimd.tensor_tensor(L["rstd"][:], L["ve"][:], mhalf[0:L["rows"], 0:G],
                                        ALU.pow).then_inc(sems[f"{kind}_rstd_set"], 1)

            def parts(p, rest, dst, left, mid, last, loaded):
                if not p.first():
                    q = p.shift(-1)
                    w(pool, f"{loaded}{q.par}", 16 * NCMB * (q.turn + 1))
                hold(pool, left, p.n + 1)
                nc.gpsimd.tensor_copy(dst[:, 1], rest[:]).then_inc(sems[mid[0]], 1)
                w(pool, mid[0], mid[1])
                nc.gpsimd.tensor_tensor(dst[:, 2], rest[:], dst[:, 1], ALU.subtract).then_inc(sems[last], 1)

            def slot(s):
                if s.back1:
                    rstd("ctx", s.back1)
                    rstd("x1", s.back1)
                    parts(s.back1, kcr, kcp, "kcr_set", ("kc1_set", s.back1.n + 1), "kc2_set", "kc_in")
                    parts(s.back1, qcr, qcp, "qcr_set", ("qc1_set", s.back1.n + 1), "qc2_set", "qc_in")
                if s.ahead:
                    rstd("x", s.ahead)
                    parts(s.ahead, qr, qp, "qkr_set", ("q1_set", 2 * s.ahead.n + 1), "q2_set", "q_in")
                    parts(s.ahead, kr, kp, "qkr_set", ("q1_set", 2 * s.ahead.n + 2), "k2_set", "k_in")

            slots(pool, slot)

            def m_rstd_step(g, first=False):
                w(pool, "m_mv_set", g + 1)
                nc.gpsimd.tensor_tensor(m_ve[:], m_mv[:, :, 1], eps_sb[:, 0:MG], ALU.add).then_inc(sems["m_ve_set"], 1)
                w(pool, "m_ve_set", g + 1)
                nc.gpsimd.tensor_tensor(m_rstd[:], m_ve[:], mhalf[:, 0:MG], ALU.pow).then_inc(sems["m_rstd_set"], 1)

            with pool.Fori(0, NGRP) as g:
                m_rstd_step(g)

        @block.vector
        def _(dve):
            for t_ in (*q_st, *k_st, *qc_st, *kc_st):
                nc.vector.memset(t_[:].bitcast(mybir.dt.uint32), 0)
            for t_ in (*v_m, *vc_m, ones_m):
                last = nc.vector.memset(t_[:], 0.0)
            last.then_inc(sems["mod_1"], 1)
            dve.wait_ge(sems["mod_1"], 1)
            for t_ in (*k_st, *kc_st):
                nc.vector.memset(t_[MROW:128], 1.0)
            for i in range(4):
                last = nc.vector.memset(ones_m[:, i, D * i:D * i + D], 1.0)
            last.then_inc(sems["z_set"], 1)

            dve.wait_ge(sems["cond_t"], 1)
            nc.vector.tensor_copy(condT[:], ps_misc[0][:, 0:B]).then_inc(sems["condT_set"], 1)
            dve.wait_ge(sems["tanh_set"], 1)
            nc.vector.tensor_scalar(tanh_c[:], tanh_c[:], 0.5, 0.5, ALU.mult, ALU.add).then_inc(sems["sig_set"], 1)
            dve.wait_ge(sems["sig_set"], 1)
            nc.vector.tensor_tensor(siluT[:], tanh_c[:], condT[:], ALU.mult).then_inc(sems["silu_set"], 1)
            dve.wait_ge(sems["mod_ps"], 1)
            dve.wait_ge(sems["b_in"], 16 * 39)
            for k in range(6):
                last = nc.vector.tensor_scalar(mod[:, k], ps_misc[0][:, k * B:(k + 1) * B], bmod_sb[:, k:k + 1],
                                               1.0 if k in (1, 4) else 0.0, ALU.add, ALU.add)
            last.then_inc(sems["mod_set"], 1)
            dve.wait_ge(sems["bo_ps"], 1)
            nc.vector.tensor_tensor(bo2[:], ps_misc[1][:, 0:2], bo_sb[:, 0:2], ALU.add).then_inc(sems["bo_set"], 1)
            dve.wait_ge(sems["bo_set"], 1)
            dve.wait_ge(sems["mod_set"], 1)
            nc.vector.tensor_scalar(gb_a[:], mod[:, 2], bo2[:, 0:1], None, ALU.mult)
            nc.vector.tensor_scalar(gb_m[:], mod[:, 5], bo_sb[:, 2:3], None, ALU.mult).then_inc(sems["gb_set"], 1)

            def stats(kind, p, src):
                L = ln[kind]
                for b in range(G):
                    last = nc.vector.bn_stats(L["stats"][:, b], src(b))
                last.then_inc(sems[f"{kind}_stats_set"], 1)

            def aggregate(kind, p):
                L = ln[kind]
                hold(dve, f"{kind}_stats_set", p.n + 1)
                for b in range(G):
                    last = nc.vector.bn_aggr(L["mv"][:, b], L["stats"][:, b])
                last.then_inc(sems[f"{kind}_mv_set"], 1)

            def normalise(kind, p, src, taken):
                L = ln[kind]
                w(dve, f"{kind}_rstd_set", p.n + 1)
                if not p.first():
                    w(dve, taken, p.n)
                for b in range(G):
                    last = nc.vector.tensor_scalar(L["xn"][:, b], src(b), L["mv"][:, b, 0:1], L["rstd"][:, b:b + 1],
                                                   ALU.subtract, ALU.mult)
                last.then_inc(sems[f"{kind}_n_set"], 1)

            def arrived(name, p, rest_at):
                if p.first():
                    dve.wait_ge(sems[f"{name}0"], 16)
                elif isinstance(p.n, int) and p.n == rest_at:
                    for n in range(1, 4):
                        dve.wait_ge(sems[f"{name}{n}"], 16)

            def x_of(p):
                return lambda b: xs[:, batch(p, b)].rearrange("t o c -> t (o c)")

            def ctx_of(p):
                return lambda b: ctx_sb[:, batch(p, b)].rearrange("t o c -> t (o c)")

            def maxima(p, u, ready, mxt, keys, done):
                b, c = divmod(u, 4)
                w(dve, ready, NU * p.n + u + 1)
                src = ps_max[u % 2][:, :].rearrange("q (j k) -> q j k", j=4)[:, :, 0:keys]
                nc.vector.reduce_max(mxt[:, b].rearrange("q (j i) -> q j i", i=4)[:, :, c], src,
                                     AX.X).then_inc(sems[done], 1)

            def minus_max(p, b, mxt, nmt, counted, high, both, taken):
                w(dve, counted, NU * p.n + 4 * b + 4)
                if not p.first():
                    w(dve, taken, 2 * p.n + b - 1)
                nc.vector.tensor_scalar(nmt[:, b, 0], mxt[:, b], -1.0, None, ALU.mult).then_inc(sems[high], 1)
                w(dve, high, 2 * p.n + b + 1)
                nc.vector.scalar_tensor_tensor(nmt[:, b, 1], mxt[:, b], -1.0, nmt[:, b, 0], ALU.mult,
                                               ALU.subtract).then_inc(sems[both], 1)

            def empty_max(p, b, job, ready, dst, name, loaded):
                w(dve, ready, 2 * p.n + b + 1)
                if not p.first():
                    q = p.shift(-1)
                    w(dve, f"{loaded}{q.par}", 16 * G * (q.turn + 1))
                nc.vector.tensor_copy(dst[:, b], ps_misc[BANK[job]][:].bitcast(bf16)[0:2 * H, 0:T]).then_inc(sems[name], 1)

            def attention_out(p, pv, den, rden_name, dst, dst_name, taken):
                w(dve, pv, NU * p.n + NU)
                nc.vector.reciprocal(den[:], ps_d[:, 0:GT]).then_inc(sems[rden_name], 1)
                w(dve, rden_name, p.n + 1)
                if not p.first():
                    w(dve, taken, p.n)
                nc.vector.tensor_tensor(dst[:], ps_o[:, 0:GT], den[:], ALU.mult).then_inc(sems[dst_name], 1)

            def rest(psum, bias, part, dst):
                return nc.vector.scalar_tensor_tensor(dst, psum, bias, part, ALU.add, ALU.subtract)

            def residual(p, ready, job, name):
                w(dve, ready, p.n + 1)
                nc.vector.tensor_tensor(xs[:, batches(p)], xs[:, batches(p)],
                                        ps_misc[BANK[job]][:, 0:GT].rearrange("t (b c) -> t b c", b=G),
                                        ALU.add).then_inc(sems[name], 1)

            def slot(s):
                a, h, d, f = s.ahead, s.here, s.back1, s.back2
                if d:
                    attention_out(d, "pv_ps", rden, "rden_set", oT, "oT_set", "proj_ps")
                for u in range(NU):
                    if h:
                        maxima(h, u, "smax_ps", mx, T, "mx_set")
                    if u == 0:
                        if f:
                            minus_max(f, 1, mxc, nmc, "mxc_set", "nmch_set", "nmc_set", "mtc_ps")
                            empty_max(f, 1, "max_c1", "mtc_ps", nmcT, "nmcT_set", "mc_in")
                        if d:
                            arrived("c_in", d, 1)
                            stats("ctx", d, ctx_of(d))
                            aggregate("ctx", d)
                    if u == 1 and d:
                        normalise("ctx", d, ctx_of(d), "ctxt_ps")
                        residual(d, "yt_ps", "y_t", "x1_set")
                        hold(dve, "x1_set", d.n + 1)
                        stats("x1", d, x_of(d))
                        aggregate("x1", d)
                    if u == 2 and d:
                        normalise("x1", d, x_of(d), "x1t_ps")
                    if u == 3:
                        if h:
                            minus_max(h, 0, mx, nm, "mx_set", "nmh_set", "nm_set", "mts_ps")
                        if d:
                            w(dve, "kvc0_set", d.n + 1)
                            if not d.first():
                                w(dve, "kc2_set", d.n)
                            rest(ps_misc[BANK["kv_c"]][:, 0:GS], bdh[:, 3:4], kcp[:, 0], kcr[:]).then_inc(sems["kcr_set"], 1)
                    if u == 4 and a:
                        arrived("x_in", a, 2 * LOOP[0])
                        stats("x", a, x_of(a))
                        aggregate("x", a)
                    if u == 5:
                        if h:
                            empty_max(h, 0, "max_s0", "mts_ps", nmT, "nmT_set", "m_in")
                        if d:
                            w(dve, "qc0_set", d.n + 1)
                            if not d.first():
                                w(dve, "qc2_set", d.n)
                            rest(ps_misc[BANK["q_c"]][:, 0:GT], bdh[:, 2:3], qcp[:, 0], qcr[:]).then_inc(sems["qcr_set"], 1)
                        if a:
                            normalise("x", a, x_of(a), "xt_ps")
                if f:
                    attention_out(f, "pvc_ps", rdenc, "rdenc_set", ocT, "ocT_set", "projc_ps")
                if h:
                    minus_max(h, 1, mx, nm, "mx_set", "nmh_set", "nm_set", "mts_ps")
                if a:
                    w(dve, "qk0_set", a.n + 1)
                    if not a.first():
                        w(dve, "q2_set", a.n)
                        w(dve, "k2_set", a.n)
                    rest(ps_misc[BANK["qk"]][:, 0:GT], bdh[:, 0:1], qp[:, 0], qr[:])
                    rest(ps_misc[BANK["qk"]][:, GT:2 * GT], bdh[:, 1:2], kp[:, 0], kr[:]).then_inc(sems["qkr_set"], 1)
                if h:
                    empty_max(h, 1, "max_s1", "mts_ps", nmT, "nmT_set", "m_in")
                for u in range(NU):
                    if d:
                        maxima(d, u, "smaxc_ps", mxc, S, "mxc_set")
                    if u == 3:
                        if f:
                            residual(f, "yct_ps", "yc_t", "x2_set")
                        if d:
                            minus_max(d, 0, mxc, nmc, "mxc_set", "nmch_set", "nmc_set", "mtc_ps")
                    if u == 6 and d:
                        empty_max(d, 0, "max_c0", "mtc_ps", nmcT, "nmcT_set", "mc_in")

            slots(dve, slot)

            def group(g):
                return bass.ds(MG * g, MG) if not isinstance(g, int) else slice(MG * g, MG * g + MG)

            def one(g, b):
                at = bass.ds(MG * g + b, 1) if not isinstance(g, int) else slice(MG * g + b, MG * g + b + 1)
                return xs[:, at].rearrange("t o c -> t (o c)")

            def m_norm(g, par, first=False):
                if not first:
                    hold(dve, "m_n_set", g)
                for b in range(MG):
                    last = nc.vector.bn_stats(m_stats[:, b], one(g, b))
                last.then_inc(sems["m_stats_set"], 1)
                hold(dve, "m_stats_set", g + 1)
                for b in range(MG):
                    last = nc.vector.bn_aggr(m_mv[:, b], m_stats[:, b])
                last.then_inc(sems["m_mv_set"], 1)
                w(dve, "m_rstd_set", g + 1)
                for b in range(MG):
                    last = nc.vector.tensor_scalar(m_n[par][:, b], one(g, b), m_mv[:, b, 0:1], m_rstd[:, b:b + 1],
                                                   ALU.subtract, ALU.mult)
                last.then_inc(sems["m_n_set"], 1)

            def m_residual(g, par, first=False):
                w(dve, "m_yt_ps", g + 1)
                if not first:
                    w(dve, f"out{par}", 16 * (g // 2) if isinstance(g, int) else 8 * (g - par))
                nc.vector.tensor_tensor(m_out[par][:], xs[:, group(g)],
                                        ps[7][:, :].rearrange("t (b c) -> t b c", b=MG), ALU.add).then_inc(sems["m_out_set"], 1)

            dve.wait_ge(sems["x2_set"], NPAIR)
            m_norm(0, 0, True)
            m_norm(1, 1)
            m_residual(0, 0, True)
            m_norm(2, 0)
            m_residual(1, 1, True)
            with dve.Fori(1, NGRP // 2 - 1) as i:
                m_norm(2 * i + 1, 1)
                m_residual(2 * i, 0)
                m_norm(2 * i + 2, 0)
                m_residual(2 * i + 1, 1)
            m_norm(NGRP - 1, 1)
            m_residual(NGRP - 2, 0)
            m_residual(NGRP - 1, 1)

        @block.scalar
        def _(act):
            act.wait_ge(sems["condT_set"], 1)
            nc.scalar.activation(tanh_c[:], condT[:], ACT.Tanh, scale=0.5).then_inc(sems["tanh_set"], 1)

            def exps(p, u, ready, src_keys, dst, name, pv):
                w(act, ready, NU * p.n + u + 1)
                if u >= 2 or not p.first():
                    w(act, pv, NU * p.n + u - 1)
                nc.scalar.activation(dst[u % 2][:].rearrange("k j q -> k (j q)"), ps_st[u % 2][0:src_keys, :],
                                     ACT.Exp, scale=SCALE).then_inc(sems[name], 1)

            def values(p, b, dst, keys, src):
                diag = dst[p.par][:, b].rearrange("t (j i) (n d) -> t j i n d", i=4, n=4)
                for i in range(4):
                    last = nc.scalar.activation(diag[:, :, i, i, :],
                                                src.rearrange("t (j i d) -> t j i d", i=4, d=D)[:, :, i, :], ACT.Copy)
                return last

            def slot(s):
                a, h, d, f = s.ahead, s.here, s.back1, s.back2
                for u in range(NU):
                    if f:
                        exps(f, u, "stc_ps", S, p_c, "expc_set", "pvc_ps")
                    if u == 0 and d:
                        w(act, "proj_ps", d.n + 1)
                        if not d.first():
                            w(act, "yt_ps", d.n)
                        for b in range(G):
                            last = nc.scalar.activation(yT[:, b * T:(b + 1) * T],
                                                        ps_misc[BANK["proj"]][:, b * T:(b + 1) * T], ACT.Identity,
                                                        bias=column(gb_a, d, b), scale=column(mod[:, 2], d, b))
                        last.then_inc(sems["y_set"], 1)
                    if u == 2 and d:
                        w(act, "ctxt_ps", d.n + 1)
                        nc.scalar.activation(cT[:], ps_misc[BANK["ctx_t"]][:, 0:GS], ACT.Copy).then_inc(sems["cT_set"], 1)
                    if u == 3 and d:
                        w(act, "kvc_ps", d.n + 1)
                        src = ps_misc[BANK["kv_c"]]
                        if not d.first():
                            q = d.shift(-1)
                            w(act, f"kc_in{q.par}", 16 * NCMB * (q.turn + 1))
                        nc.scalar.activation(kcp[:, 0], src[:, 0:GS], ACT.Identity, bias=bdh[:, 3:4])
                        if not d.first(2):
                            w(act, "pvc_ps", NU * (d.n - 1))
                        for b in range(G):
                            last = values(d, b, vc_m, S, src[0:S, GS + b * C:GS + (b + 1) * C])
                        last.then_inc(sems["kvc0_set"], 1)
                    if u == 4 and d:
                        w(act, "x1t_ps", d.n + 1)
                        nc.scalar.activation(x1T[:], ps_misc[BANK["x1_t"]][:, 0:GT], ACT.Copy).then_inc(sems["x1T_set"], 1)
                    if u == 5 and d:
                        w(act, "qc_ps", d.n + 1)
                        if not d.first():
                            q = d.shift(-1)
                            w(act, f"qc_in{q.par}", 16 * NCMB * (q.turn + 1))
                        nc.scalar.activation(qcp[:, 0], ps_misc[BANK["q_c"]][:, 0:GT], ACT.Identity,
                                             bias=bdh[:, 2:3]).then_inc(sems["qc0_set"], 1)
                    if u == 6 and a:
                        w(act, "xt_ps", a.n + 1)
                        if a.first():
                            act.wait_ge(sems["gb_set"], 1)
                        for b in range(G):
                            last = nc.scalar.activation(xmT[:, b * T:(b + 1) * T],
                                                        ps_misc[BANK["x_t"]][:, b * T:(b + 1) * T], ACT.Identity,
                                                        bias=column(mod[:, 0], a, b), scale=column(mod[:, 1], a, b))
                        last.then_inc(sems["xmT_set"], 1)
                    if u == 7 and a:
                        w(act, "qk_ps", a.n + 1)
                        src = ps_misc[BANK["qk"]]
                        if not a.first():
                            q = a.shift(-1)
                            w(act, f"q_in{q.par}", 16 * NCMB * (q.turn + 1))
                            w(act, f"k_in{q.par}", 16 * NCMB * (q.turn + 1))
                        nc.scalar.activation(qp[:, 0], src[:, 0:GT], ACT.Identity, bias=bdh[:, 0:1])
                        nc.scalar.activation(kp[:, 0], src[:, GT:2 * GT], ACT.Identity,
                                             bias=bdh[:, 1:2]).then_inc(sems["qk0_set"], 1)
                for u in range(NU):
                    if h:
                        exps(h, u, "st_ps", T, p_s, "exp_set", "pv_ps")
                    if u == 1:
                        if f:
                            w(act, "projc_ps", f.n + 1)
                            if not f.first():
                                w(act, "yct_ps", f.n)
                            nc.scalar.activation(ycT[:], ps_misc[BANK["proj_c"]][:, 0:GT], ACT.Identity,
                                                 bias=bo2[:, 1:2]).then_inc(sems["yc_set"], 1)
                        if a:
                            w(act, "v_ps", a.n + 1)
                            if not a.first(2):
                                w(act, "pv_ps", NU * (a.n - 1))
                            for b in range(G):
                                last = values(a, b, v_m, T, ps_misc[BANK["v"]][:, b * C:(b + 1) * C])
                            last.then_inc(sems["v_set"], 1)

            slots(act, slot)

            def one(tile, g, b):
                return tile[:, bass.ds(MG * g + b, 1) if not isinstance(g, int) else slice(MG * g + b, MG * g + b + 1)]

            def m_modulate(g, par, first=False):
                w(act, "m_nt_ps", g + 1)
                for b in range(MG):
                    last = nc.scalar.activation(m_nT[par][:, b * T:(b + 1) * T], ps[0][:, b * T:(b + 1) * T], ACT.Identity,
                                                bias=one(mod[:, 3], g, b), scale=one(mod[:, 4], g, b))
                last.then_inc(sems["m_nT_set"], 1)

            def m_gelu(g, par, first=False):
                for k in range(NF):
                    w(act, "m_h_ps", NF * g + k + 1)
                    nc.scalar.activation(hT[par][:, k], ps[2 + k][:, :], ACT.Gelu_apprx_tanh,
                                         bias=b1_sb[:, k:k + 1]).then_inc(sems["m_hT_set"], 1)

            def m_gate(g, par, first=False):
                w(act, "m_y_ps", g + 1)
                for b in range(MG):
                    last = nc.scalar.activation(m_y[par][:, b * T:(b + 1) * T], ps[6][:, b * T:(b + 1) * T], ACT.Identity,
                                                bias=one(gb_m, g, b), scale=one(mod[:, 5], g, b))
                last.then_inc(sems["m_y_set"], 1)

            m_modulate(0, 0, True)
            with act.Fori(0, NGRP // 2 - 1) as i:
                for k in range(2):
                    m_modulate(2 * i + k + 1, (k + 1) % 2)
                    m_gelu(2 * i + k, k)
                    m_gate(2 * i + k, k)
            m_modulate(NGRP - 1, 1)
            m_gelu(NGRP - 2, 0)
            m_gate(NGRP - 2, 0)
            m_gelu(NGRP - 1, 1)
            m_gate(NGRP - 1, 1)

        @block.tensor
        def _(pe):
            mm, tr = nc.tensor.matmul, nc.tensor.transpose

            pe.wait_ge(sems["id_set"], 1)
            pe.wait_ge(sems["w_in"], 16 * 9)
            tr(ps_misc[0][:, 0:B], cond_sb[:], ident[0:B, 0:B]).then_inc(sems["cond_t"], 1)
            pe.wait_ge(sems["b_in"], 16 * 39)
            mm(ps_misc[1][:, 0:1], wproj_sb[:], bv_sb[:, 0:1], start=True, stop=True)
            mm(ps_misc[1][:, 1:2], wcproj_sb[:], bv_sb[:, 1:2], start=True, stop=True).then_inc(sems["bo_ps"], 1)
            pe.wait_ge(sems["silu_set"], 1)
            for k in range(6):
                last = mm(ps_misc[0][:, k * B:(k + 1) * B], wmod_sb[:, k * C:(k + 1) * C], siluT[:], start=True, stop=True)
            last.then_inc(sems["mod_ps"], 1)
            pe.wait_ge(sems["gb_set"], 1)
            pe.wait_ge(sems["wdh_set"], 4)
            pe.wait_ge(sems["z_set"], 1)

            def bank(s, name):
                before = s.job_before(name)
                if before:
                    job, p = before
                    name_, count = EMPTIED[job]
                    w(pe, name_, count(p))
                return ps_misc[BANK[name]]

            def scores(p, u, qt, kt, keys, counted):
                b, c = divmod(u, 4)
                dst = ps_max[u % 2]
                for j in range(4):
                    h = 4 * j + c
                    last = mm(dst[:, j * T:j * T + keys], qt[p.par][0:KMAX, h, b * T:(b + 1) * T],
                              kt[p.par][0:KMAX, h, b * keys:(b + 1) * keys], start=True, stop=True)
                last.then_inc(sems[counted], 1)

            def scores_t(p, u, qt, kt, keys, counted):
                b, c = divmod(u, 4)
                dst = ps_st[u % 2]
                for j in range(4):
                    h = 4 * j + c
                    last = mm(dst[0:keys, j * T:(j + 1) * T], kt[p.par][:, h, b * keys:(b + 1) * keys],
                              qt[p.par][:, h, b * T:(b + 1) * T], start=True, stop=True)
                last.then_inc(sems[counted], 1)

            def values(p, u, probs, vt, keys, counted):
                b, c = divmod(u, 4)
                for dst, ones in ((ps_o, False), (ps_d, True)):
                    for j in range(4):
                        lhs = ones_m[0:keys, c] if ones else vt[p.par][:, b, 4 * j + c]
                        last = mm(dst[32 * j:32 * j + 32, b * T:(b + 1) * T], lhs, probs[u % 2][:, j],
                                  start=(c == 0), stop=(c == 3))
                last.then_inc(sems[counted], 1)

            def slot(s):
                a, h, d, f = s.ahead, s.here, s.back1, s.back2
                was = s.before()

                def max_self(u):
                    if u == 0:
                        w(pe, f"q_in{h.par}", 16 * NCMB * (h.turn + 1))
                        w(pe, f"k_in{h.par}", 16 * NCMB * (h.turn + 1))
                        if was.back1:
                            w(pe, "mxc_set", NU * was.back1.n + NU)
                        elif was.here:
                            w(pe, "mx_set", NU * was.here.n + NU)
                    elif u >= 2:
                        w(pe, "mx_set", NU * h.n + u - 1)
                    scores(h, u, q_st, k_st, T, "smax_ps")

                def max_cross(u):
                    if u == 0:
                        w(pe, f"qc_in{d.par}", 16 * NCMB * (d.turn + 1))
                        w(pe, f"kc_in{d.par}", 16 * NCMB * (d.turn + 1))
                        if h:
                            w(pe, "mx_set", NU * h.n + NU)
                        elif was.back1:
                            w(pe, "mxc_set", NU * was.back1.n + NU)
                    elif u >= 2:
                        w(pe, "mxc_set", NU * d.n + u - 1)
                    scores(d, u, qc_st, kc_st, S, "smaxc_ps")

                def st_cross(u):
                    if u % 4 == 0:
                        w(pe, f"mc_in{f.par}", 16 * (G * f.turn + u // 4 + 1))
                    if u < 2:
                        if was.here:
                            w(pe, "exp_set", NU * was.here.n + NU - 1 + u)
                        elif was.back2:
                            w(pe, "expc_set", NU * was.back2.n + NU - 1 + u)
                    else:
                        w(pe, "expc_set", NU * f.n + u - 1)
                    scores_t(f, u, qc_st, kc_st, S, "stc_ps")

                def st_self(u):
                    if u % 4 == 0:
                        w(pe, f"m_in{h.par}", 16 * (G * h.turn + u // 4 + 1))
                    if u < 2:
                        if f:
                            w(pe, "expc_set", NU * f.n + NU - 1 + u)
                        elif was.here:
                            w(pe, "exp_set", NU * was.here.n + NU - 1 + u)
                    else:
                        w(pe, "exp_set", NU * h.n + u - 1)
                    scores_t(h, u, q_st, k_st, T, "st_ps")

                def pv_cross(u):
                    if u == 0 and was.here:
                        w(pe, "oT_set", was.here.n + 1)
                    elif u == 0 and was.back2:
                        w(pe, "ocT_set", was.back2.n + 1)
                    w(pe, "expc_set", NU * f.n + u + 1)
                    values(f, u, p_c, vc_m, S, "pvc_ps")

                def pv_self(u):
                    if u == 0 and f:
                        w(pe, "ocT_set", f.n + 1)
                    elif u == 0 and was.here:
                        w(pe, "oT_set", was.here.n + 1)
                    w(pe, "exp_set", NU * h.n + u + 1)
                    if u == 0:
                        w(pe, "v_set", h.n + 1)
                    values(h, u, p_s, v_m, T, "pv_ps")

                def transposed(job, kind, p, rows, counted):
                    dst = bank(s, job)
                    w(pe, f"{kind}_n_set", p.n + 1)
                    for b in range(G):
                        last = tr(dst[:, b * rows:(b + 1) * rows], ln[kind]["xn"][:, b], ident[0:rows, 0:rows])
                    last.then_inc(sems[counted], 1)

                def back(job, p, src, ready, counted):
                    dst = bank(s, job)
                    w(pe, ready, p.n + 1)
                    for b in range(G):
                        last = tr(dst[:, b * C:(b + 1) * C], src[:, b * T:(b + 1) * T], ident[:])
                    last.then_inc(sems[counted], 1)

                def project(job, p, weights, src, ready, counted, cols=GT):
                    dst = bank(s, job)
                    w(pe, ready, p.n + 1)
                    mm(dst[:, 0:cols], weights, src, start=True, stop=True).then_inc(sems[counted], 1)

                def max_t(job, p, b, src, ready, counted):
                    dst = bank(s, job)
                    w(pe, ready, 2 * p.n + b + 1)
                    tr(dst[:].bitcast(bf16)[0:2 * H, 0:T], src[:, b].rearrange("q r h -> q (r h)"),
                       ident16[:]).then_inc(sems[counted], 1)

                for u in range(NU):
                    if h:
                        max_self(u)
                    if f:
                        st_cross(u)
                        if u:
                            pv_cross(u - 1)
                    if u == 0:
                        if d:
                            project("proj", d, wproj_sb[:], oT[:], "oT_set", "proj_ps")
                        if f:
                            max_t("max_c1", f, 1, nmc, "nmc_set", "mtc_ps")
                    if u == 1 and d:
                        back("y_t", d, yT, "y_set", "yt_ps")
                    if u == 2 and d:
                        transposed("ctx_t", "ctx", d, S, "ctxt_ps")
                    if u == 3 and d:
                        dst = bank(s, "kv_c")
                        w(pe, "cT_set", d.n + 1)
                        mm(dst[:, 0:GS], wdh[:, 3], cT[:], start=True, stop=True)
                        for b in range(G):
                            last = mm(dst[0:S, GS + b * C:GS + (b + 1) * C], cT[:, b * S:(b + 1) * S], wkvc_sb[:, C:2 * C],
                                      start=True, stop=True)
                        last.then_inc(sems["kvc_ps"], 1)
                    if u == 4 and d:
                        transposed("x1_t", "x1", d, T, "x1t_ps")
                    if u == 5:
                        if h:
                            max_t("max_s0", h, 0, nm, "nm_set", "mts_ps")
                        if d:
                            project("q_c", d, wdh[:, 2], x1T[:], "x1T_set", "qc_ps")
                    if u == 6 and a:
                        transposed("x_t", "x", a, T, "xt_ps")
                    if u == 7:
                        if f:
                            pv_cross(7)
                        if a:
                            dst = bank(s, "qk")
                            w(pe, "xmT_set", a.n + 1)
                            mm(dst[:, 0:GT], wdh[:, 0], xmT[:], start=True, stop=True)
                            mm(dst[:, GT:2 * GT], wdh[:, 1], xmT[:], start=True, stop=True).then_inc(sems["qk_ps"], 1)
                for u in range(NU):
                    if h:
                        st_self(u)
                        if u:
                            pv_self(u - 1)
                    if d:
                        max_cross(u)
                    if u == 0 and h:
                        max_t("max_s1", h, 1, nm, "nm_set", "mts_ps")
                    if u == 1:
                        if f:
                            project("proj_c", f, wcproj_sb[:], ocT[:], "ocT_set", "projc_ps")
                        if a:
                            dst = bank(s, "v")
                            for b in range(G):
                                last = mm(dst[:, b * C:(b + 1) * C], xmT[:, b * T:(b + 1) * T], wqkv_sb[:, 2 * C:3 * C],
                                          start=True, stop=True)
                            last.then_inc(sems["v_ps"], 1)
                    if u == 2 and f:
                        back("yc_t", f, ycT, "yc_set", "yct_ps")
                    if u == 6 and d:
                        max_t("max_c0", d, 0, nmc, "nmc_set", "mtc_ps")
                if h:
                    pv_self(7)

            slots(pe, slot)

            def m_transpose(g, par, first=False):
                w(pe, "m_n_set", g + 1)
                if not first:
                    w(pe, "m_nT_set", g)
                for b in range(MG):
                    last = tr(ps[0][:, b * T:(b + 1) * T], m_n[par][:, b], ident[:])
                last.then_inc(sems["m_nt_ps"], 1)

            def m_up(g, par, first=False):
                w(pe, "m_nT_set", g + 1)
                for k in range(NF):
                    if not first:
                        w(pe, "m_hT_set", NF * g - NF + k + 1)
                    mm(ps[2 + k][:, :], w1_sb[:, k * 128:(k + 1) * 128], m_nT[par][:], start=True,
                       stop=True).then_inc(sems["m_h_ps"], 1)

            def m_down(g, par, first=False):
                if not first:
                    w(pe, "m_y_set", g)
                for k in range(NF):
                    w(pe, "m_hT_set", NF * g + k + 1)
                    last = mm(ps[6][:, :], w2_sb[:, k], hT[par][:, k], start=(k == 0), stop=(k == NF - 1))
                last.then_inc(sems["m_y_ps"], 1)

            def m_back(g, par, first=False):
                w(pe, "m_y_set", g + 1)
                if not first:
                    w(pe, "m_out_set", g)
                for b in range(MG):
                    last = tr(ps[7][:, b * C:(b + 1) * C], m_y[par][:, b * T:(b + 1) * T], ident[:])
                last.then_inc(sems["m_yt_ps"], 1)

            pe.wait_ge(sems["x2_set"], NPAIR)
            m_transpose(0, 0, True)
            m_up(0, 0, True)
            m_transpose(1, 1)
            m_down(0, 0, True)
            m_up(1, 1)
            m_back(0, 0, True)
            m_transpose(2, 0)
            m_down(1, 1)
            with pe.Fori(1, NGRP // 2 - 1) as i:
                for k in range(2):
                    m_up(2 * i + k, k)
                    m_back(2 * i + k - 1, (k + 1) % 2)
                    m_transpose(2 * i + k + 1, (k + 1) % 2)
                    m_down(2 * i + k, k)
            m_up(NGRP - 2, 0)
            m_back(NGRP - 3, 1)
            m_transpose(NGRP - 1, 1)
            m_down(NGRP - 2, 0)
            m_up(NGRP - 1, 1)
            m_back(NGRP - 2, 0)
            m_down(NGRP - 1, 1)
            m_back(NGRP - 1, 1)


_INS = ["x", "cond_1024", "ctx_1024"] + ["L0_xcond_" + n for n in (
    "W_mod", "b_mod", "W_qkv", "b_qkv", "W_proj", "b_proj", "W_qc", "b_qc", "W_kvc", "b_kvc", "W_cproj", "b_cproj",
    "W_mlp1", "b_mlp1", "W_mlp2", "b_mlp2")]


def kernel(**inputs):
    import numpy as np
    import concourse.bacc as bacc
    from concourse.bass_utils import run_bass_kernel_spmd

    nc = bacc.Bacc("TRN2", target_bir_lowering=False, num_devices=1)
    arrays, args = {}, []
    for name in _INS:
        a = np.ascontiguousarray(inputs[name])
        arrays[name] = a
        args.append(nc.dram_tensor(name, a.shape, mybir.dt.from_np(a.dtype), kind="ExternalInput").ap())
    args.append(nc.dram_tensor("out", (B, T, C), mybir.dt.float32, kind="ExternalOutput").ap())
    block_kernel(nc, *args)
    r = run_bass_kernel_spmd(nc, [arrays], core_ids=[0])
    return r.results[0]["out"]
```

```python
from contextlib import ExitStack

import concourse.bass as bass
from concourse import mybir

B, T, C = 32, 128, 128
H, D = 16, 8
S = 77
F = 512
G = 2
NPAIR = B // G
GT, GS = G * T, G * S
NF = F // 128
MG = 4
NGRP = B // MG
NU = 8
TICKS = 2 * NU
EPS = 1e-6
SCALE = float(D) ** -0.5
COMBOS = [(0, 0), (0, 1), (0, 2), (1, 0), (1, 1), (2, 0)]
NCMB = len(COMBOS)
ZROW = D * NCMB
MROW = 126


def self_max(t):
    return ("here", t) if t < NU else None


def self_exp(t):
    return ("here", t - NU) if t >= NU else None


def self_pv(t):
    return ("here", t - NU - 1) if t > NU else ("back1", NU - 1) if t == 0 else None


def cross_max(t):
    return ("back2", t - NU) if t >= NU else None


def cross_exp(t):
    return ("back3", t) if t < NU else None


def cross_pv(t):
    return ("back3", t - 1) if 1 <= t <= NU else None


def ring(*streams):
    return [(n, *f(t)) for t in range(TICKS) for n, f in streams if f(t)]


MAX_RING = ring(("self", self_max), ("cross", cross_max))
EXP_RING = ring(("self", self_exp), ("cross", cross_exp))

MISC = [("max_c1", "back3", 0), ("ctx_t", "back1", 1), ("o_t", "back1", 0), ("x_t", "ahead", 1),
        ("ob_t", "back1", 0), ("max_s0", "here", 1), ("qk", "ahead", 0), ("proj", "back1", 1), ("y_t", "back1", 1),
        ("max_s1", "here", 0), ("kv_c", "back1", 1), ("oc_t", "back3", 0), ("v", "ahead", 0),
        ("obc_t", "back3", 0), ("x1_t", "back1", 1), ("max_c0", "back2", 1), ("proj_c", "back3", 0),
        ("q_c", "back1", 1), ("yc_t", "back3", 0)]
BANK = {name: bank for name, _, bank in MISC}


class Pair:

    def __init__(self, i, k):
        self.i, self.k = i, k
        self.n = 2 * i + k
        self.par = k % 2
        self.turn = i + k // 2

    def exists(self):
        return not isinstance(self.n, int) or 0 <= self.n < NPAIR

    def first(self, m=1):
        return isinstance(self.n, int) and self.n < m

    def shift(self, d):
        return Pair(self.i, self.k + d)


class Slot:
    def __init__(self, i, k):
        here = Pair(i, k)
        self.pairs = {"ahead": here.shift(1), "here": here,
                      "back1": here.shift(-1), "back2": here.shift(-2), "back3": here.shift(-3)}
        self.i, self.k = i, k

    def pair(self, whose):
        p = self.pairs[whose]
        return p if p.exists() else None

    def unit(self, use):
        return (self.pair(use[0]), use[1]) if use and self.pair(use[0]) else None

    def before(self):
        return Slot(self.i, self.k - 1)

    def bank_before(self, uses, stream, u):
        at = next(n for n, (name, _, unit) in enumerate(uses) if (name, unit) == (stream, u))
        bank, slot = at % 2, self
        for _ in range(3 * len(uses)):
            at -= 2
            if at < 0:
                slot, at = slot.before(), at + len(uses)
            name, whose, unit = uses[at]
            if slot.pairs[whose].exists():
                return bank, (name, slot.pairs[whose], unit)
        return bank, None

    def job_before(self, name):
        names = [m[0] for m in MISC]
        slot, at = self, names.index(name)
        for _ in range(4 * len(MISC)):
            at -= 1
            if at < 0:
                slot, at = slot.before(), len(MISC) - 1
            job, whose, bank = MISC[at]
            if bank == BANK[name] and slot.pairs[whose].exists():
                return job, slot.pairs[whose]
        return None


FIRST_SLOT, LAST_SLOT = -1, NPAIR + 2
LOOP = (2, (NPAIR - 2) // 2)


def slots(engine, emit):
    for s in range(FIRST_SLOT, 2 * LOOP[0]):
        emit(Slot(s // 2, s % 2))
    with engine.Fori(LOOP[0], LOOP[1]) as i:
        emit(Slot(i, 0))
        emit(Slot(i, 1))
    for s in range(2 * LOOP[1], LAST_SLOT + 1):
        emit(Slot(s // 2, s % 2))


def block_kernel(nc, x, cond, ctx, w_mod, b_mod, w_qkv, b_qkv, w_proj, b_proj, w_qc, b_qc, w_kvc, b_kvc,
                 w_cproj, b_cproj, w_mlp1, b_mlp1, w_mlp2, b_mlp2, out):
    f32, bf16 = mybir.dt.float32, mybir.dt.bfloat16
    ALU, ACT, AX = mybir.AluOpType, mybir.ActivationFunctionType, mybir.AxisListType

    es = ExitStack()
    with es:
        def sb(name, shape, dt=f32):
            return es.enter_context(nc.sbuf_tensor(name, shape, dt))

        def pairbuf(name, shape, dt=f32):
            return [sb(f"{name}{i}", shape, dt) for i in range(2)]

        sems = {}

        def sem(name):
            sems[name] = es.enter_context(nc.semaphore(name))
            return sems[name]

        xs = sb("xs", [T, B, C])
        ctx_sb = sb("ctx_sb", [S, B, C])
        cond_sb = sb("cond_sb", [B, C])
        wmod_sb = sb("wmod_sb", [C, 6 * C])
        wqkv_sb = sb("wqkv_sb", [C, 3 * C])
        wproj_sb = sb("wproj_sb", [C, C])
        wqc_sb = sb("wqc_sb", [C, C])
        wkvc_sb = sb("wkvc_sb", [C, 2 * C])
        wcproj_sb = sb("wcproj_sb", [C, C])
        w1_sb = sb("w1_sb", [C, F])
        w2_sb = sb("w2_sb", [128, NF, C])
        wdh = sb("wdh", [C, 4, C])
        bmod_sb = sb("bmod_sb", [C, 6])
        bdh = sb("bdh", [C, 4])
        bv_sb = sb("bv_sb", [C, 2])
        bo_sb = sb("bo_sb", [C, 3])
        b1_sb = sb("b1_sb", [128, NF])
        bo2 = sb("bo2", [C, 2])
        ident = sb("ident", [128, 128])
        ident16 = sb("ident16", [128, 128], bf16)
        condT = sb("condT", [C, B])
        tanh_c = sb("tanh_c", [C, B])
        siluT = sb("siluT", [C, B])
        mod = sb("mod", [C, 6, B])
        gb_a = sb("gb_a", [C, B])
        gb_m = sb("gb_m", [C, B])
        eps_sb = sb("eps_sb", [128, MG])
        mhalf = sb("mhalf", [128, MG])

        qk_st = pairbuf("qk_st", [128, H, 2, GT], bf16)
        qkc_st = pairbuf("qkc_st", [128, H, 2, GT], bf16)
        v_m = pairbuf("v_m", [T, G, H, 32])
        vc_m = pairbuf("vc_m", [T, G, H, 32])
        ln = {}
        for kind, rows in (("x", T), ("ctx", S), ("x1", T)):
            ln[kind] = dict(rows=rows, stats=sb(f"{kind}_stats", [rows, G, 6]), mv=sb(f"{kind}_mv", [rows, G, 2]),
                            ve=sb(f"{kind}_ve", [rows, G]), rstd=sb(f"{kind}_rstd", [rows, G]),
                            xn=sb(f"{kind}_n", [rows, G, C]))
        xmT = sb("xmT", [C, GT])
        cT = sb("cT", [C, GS])
        x1T = sb("x1T", [C, GT])
        qkp = sb("qkp", [C, 2, 3, GT], bf16)
        qkcp = sb("qkcp", [C, 2, 3, GT], bf16)
        qkr = sb("qkr", [C, 2, GT])
        qcr = sb("qcr", [C, GT])
        kcr = sb("kcr", [C, GS])
        mx = sb("mx", [T, G, H])
        mxc = sb("mxc", [T, G, H])
        nm = sb("nm", [T, G, 2, H], bf16)
        nmc = sb("nmc", [T, G, 2, H], bf16)
        nmT = sb("nmT", [2 * H, G, T], bf16)
        nmcT = sb("nmcT", [2 * H, G, T], bf16)
        p_s = [sb(f"p_s{i}", [T, 4, T]) for i in range(2)]
        p_c = [sb(f"p_c{i}", [T, 4, T]) for i in range(2)]
        att = {}
        for kind in ("s", "c"):
            att[kind] = dict(sum=sb(f"{kind}_sum", [128, G, 2, T]),
                             rden=sb(f"{kind}_rden", [T, 2 * G, 8]),
                             o=sb(f"{kind}_o", [T, 2 * G, 8, D]))
        oT = sb("oT", [C, GT])
        ocT = sb("ocT", [C, GT])
        yT = sb("yT", [C, GT])
        ycT = sb("ycT", [C, GT])

        m_stats = sb("m_stats", [T, MG, 6])
        m_mv = sb("m_mv", [T, MG, 2])
        m_ve = sb("m_ve", [T, MG])
        m_rstd = sb("m_rstd", [T, MG])
        m_n = pairbuf("m_n", [T, MG, C])
        m_nT = pairbuf("m_nT", [C, MG * T])
        hT = [t[:].rearrange("p h a t -> p (h a t)").bitcast(f32)[:, 0:NF * MG * T].rearrange(
            "p (k t) -> p k t", k=NF) for t in qk_st]
        m_y = pairbuf("m_y", [C, MG * T])
        m_out = pairbuf("m_out", [T, MG, C])

        ps = [es.enter_context(nc.psum_tensor(f"ps{i}", [128, 512], f32)) for i in range(8)]
        ps_max, ps_st, ps_o, ps_oc, ps_misc = ps[0:2], ps[2:4], ps[4], ps[5], ps[6:8]

        for name in ("w_in wm_in wq_in b_in x_in0 x_in1 x_in2 x_in3 c_in0 c_in1 c_in2 c_in3 z_pool z_dve zq_set zk_set zv_set zs1_in zc0_in zc1_in "
                     "pad_set id_set wdh_set cond_t condT_set "
                     "tanh_set sig_set silu_set mod_ps mod_set bo_ps bo_set gb_set "
                     "xt_ps qk_ps v_ps ctxt_ps kvc_ps proj_ps yt_ps x1t_ps qc_ps projc_ps yct_ps mts_ps mtc_ps "
                     "smax_ps smaxc_ps st_ps stc_ps pv_ps pvc_ps ot_ps obt_ps oct_ps obct_ps "
                     "xmT_set qk0_set v_set cT_set kvc0_set y_set x1T_set qc0_set yc_set exp_set expc_set "
                     "sum_set sumc_set oT_set ocT_set "
                     "qkr_set kcr_set qcr_set mx_set mxc_set nmh_set nm_set nmch_set nmc_set nmT_set "
                     "nmcT_set rden_set o_set rdenc_set oc_set x1_set x2_set "
                     "qk1_set qk2_set kc1_set kc2_set qc1_set qc2_set "
                     "qk_in0 qk_in1 qkc_in0 qkc_in1 m_in0 m_in1 mc_in0 mc_in1 "
                     "m_stats_set m_mv_set m_ve_set m_rstd_set m_n_set m_nt_ps m_nT_set m_h_ps m_hT_set m_y_ps "
                     "m_y_set m_yt_ps m_out_set out0 out1").split():
            sem(name)
        for name in ("SP", "Pool", "DVE"):
            sem(f"held_{name}")
        for kind in ln:
            for what in ("stats", "mv", "ve", "rstd", "n"):
                sem(f"{kind}_{what}_set")

        def w(eng, name, value):
            eng.wait_ge(sems[name], value)

        def hold(eng, name, value):
            eng.wait_ge(sems[name], value)
            eng.sem_inc(sems[f"held_{eng.engine.name}"], 1)

        EMPTIED = {"proj": ("y_set", lambda p: p.n + 1), "max_c1": ("nmcT_set", lambda p: 2 * p.n + 2),
                   "y_t": ("x1_set", lambda p: p.n + 1), "ctx_t": ("cT_set", lambda p: p.n + 1),
                   "kv_c": ("kcr_set", lambda p: p.n + 1), "x1_t": ("x1T_set", lambda p: p.n + 1),
                   "max_s0": ("nmT_set", lambda p: 2 * p.n + 1), "q_c": ("qcr_set", lambda p: p.n + 1),
                   "x_t": ("xmT_set", lambda p: p.n + 1), "qk": ("qkr_set", lambda p: p.n + 1),
                   "max_s1": ("nmT_set", lambda p: 2 * p.n + 2), "proj_c": ("yc_set", lambda p: p.n + 1),
                   "v": ("v_set", lambda p: p.n + 1), "yc_t": ("x2_set", lambda p: p.n + 1),
                   "max_c0": ("nmcT_set", lambda p: 2 * p.n + 1), "o_t": ("o_set", lambda p: p.n + 1),
                   "ob_t": ("oT_set", lambda p: p.n + 1), "oc_t": ("oc_set", lambda p: p.n + 1),
                   "obc_t": ("ocT_set", lambda p: p.n + 1)}

        def batch(p, b):
            return bass.ds(2 * p.n + b, 1) if not isinstance(p.n, int) else slice(2 * p.n + b, 2 * p.n + b + 1)

        def batches(p):
            return bass.ds(2 * p.n, G) if not isinstance(p.n, int) else slice(2 * p.n, 2 * p.n + G)

        def column(tile, p, b):
            return tile[:, batch(p, b)]

        key_parts = [qkcp[:, 1, n].rearrange("c (b k) -> c b k", b=G)[:, :, 0:S] for n in range(3)]
        u32 = mybir.dt.uint32

        block = es.enter_context(nc.Block())

        @block.sync
        def _(sp):
            def o_rows(src):
                return src.rearrange("(j r m) c -> r j m c", r=2, m=2 * D)

            q4 = B // 4

            def load(n):
                sp.dma_start(xs[:, n * q4:(n + 1) * q4],
                             x[n * q4:(n + 1) * q4].rearrange("b t c -> t b c")).then_inc(sems[f"x_in{n}"], 16)
                sp.dma_start(ctx_sb[:, n * q4:(n + 1) * q4],
                             ctx[n * q4:(n + 1) * q4].rearrange("b t c -> t b c")).then_inc(sems[f"c_in{n}"], 16)

            sp.dma_start(cond_sb[:], cond).then_inc(sems["wm_in"], 16)
            sp.dma_start(wmod_sb[:], w_mod).then_inc(sems["wm_in"], 16)
            load(0)
            for dst, src in ((wqkv_sb, w_qkv), (wqc_sb, w_qc), (wkvc_sb, w_kvc)):
                sp.dma_start(dst[:], src).then_inc(sems["wq_in"], 16)
            with nc.allow_non_contiguous_dma(reason="bias columns"):
                sp.dma_start(bmod_sb[:], b_mod.rearrange("(k c) -> c k", k=6)).then_inc(sems["b_in"], 16)
                for n, (src, at) in enumerate(((b_qkv, 0), (b_qkv, C), (b_qc, 0), (b_kvc, 0))):
                    for d in range(D):
                        sp.dma_start(bdh[d * H:(d + 1) * H, n:n + 1],
                                     src[at + d:at + C:D].rearrange("(h o) -> h o", o=1)).then_inc(sems["b_in"], 16)
                for n, (src, at) in enumerate(((b_qkv, 2 * C), (b_kvc, C))):
                    for r in range(2):
                        sp.dma_start(bv_sb[r * C // 2:(r + 1) * C // 2, n:n + 1],
                                     o_rows(src[at:at + C].rearrange("(c o) -> c o", o=1))[r]).then_inc(sems["b_in"], 16)
                for n, src in enumerate((b_proj, b_cproj, b_mlp2)):
                    sp.dma_start(bo_sb[:, n:n + 1], src.rearrange("(c o) -> c o", o=1)).then_inc(sems["b_in"], 16)
                sp.dma_start(b1_sb[:], b_mlp1.rearrange("(k c) -> c k", k=NF)).then_inc(sems["b_in"], 16)
            for dst, src in ((wproj_sb, w_proj), (wcproj_sb, w_cproj)):
                for r in range(2):
                    sp.dma_start(dst[r * C // 2:(r + 1) * C // 2], o_rows(src)[r]).then_inc(sems["w_in"], 16)
            sp.dma_start(w1_sb[:], w_mlp1).then_inc(sems["w_in"], 16)
            sp.dma_start(w2_sb[:], w_mlp2.rearrange("(k f) c -> f k c", k=NF)).then_inc(sems["w_in"], 16)
            for n in range(1, 4):
                load(n)

            def stack(dst, parts, name):
                for c, (a, b) in enumerate(COMBOS):
                    sp.dma_start(dst[D * c:D * c + D], parts[:].rearrange("c a p t -> c (a p) t")[:, a:b + 4:b + 3 - a]
                                 ).then_inc(sems[name], 16)

            def max_rows(dst, b, src, name):
                sp.dma_start(dst[MROW:MROW + 2, :, 0, b * T:(b + 1) * T], src[:, b]).then_inc(sems[name], 16)

            def slot(s):
                a, h, f, e = (s.pair(n) for n in ("ahead", "here", "back2", "back3"))
                if e:
                    w(sp, "nmcT_set", 2 * e.n + 2)
                    max_rows(qkc_st[e.par], 1, nmcT, f"mc_in{e.par}")
                if f:
                    if f.first(2):
                        w(sp, f"zc{f.par}_in", 16 * 5)
                    hold(sp, "kc2_set", f.n + 1)
                    hold(sp, "qc2_set", f.n + 1)
                    if not f.first(2):
                        w(sp, "stc_ps", NU * (f.n - 1))
                    stack(qkc_st[f.par], qkcp, f"qkc_in{f.par}")
                if h:
                    w(sp, "nmT_set", 2 * h.n + 1)
                    max_rows(qk_st[h.par], 0, nmT, f"m_in{h.par}")
                    w(sp, "nmT_set", 2 * h.n + 2)
                    max_rows(qk_st[h.par], 1, nmT, f"m_in{h.par}")
                if a:
                    if a.first(2) and a.n == 1:
                        w(sp, "zs1_in", 16 * 2)
                    hold(sp, "qk2_set", a.n + 1)
                    if not a.first(2):
                        w(sp, "st_ps", NU * (a.n - 1))
                    stack(qk_st[a.par], qkp, f"qk_in{a.par}")
                if f:
                    w(sp, "nmcT_set", 2 * f.n + 1)
                    max_rows(qkc_st[f.par], 0, nmcT, f"mc_in{f.par}")

            w(sp, "zq_set", 1)
            w(sp, "zk_set", 1)
            sp.dma_start(qk_st[1][ZROW:MROW], qk_st[0][ZROW:MROW]).then_inc(sems["zs1_in"], 16)
            sp.dma_start(qk_st[1][MROW:128, :, 1], qk_st[0][MROW:128, :, 1]).then_inc(sems["zs1_in"], 16)
            for par in range(2):
                done = sems[f"zc{par}_in"]
                sp.dma_start(qkc_st[par][ZROW:MROW], qk_st[0][ZROW:MROW]).then_inc(done, 16)
                for b in range(G):
                    sp.dma_start(qkc_st[par][MROW:128, :, 1, b * T:b * T + S],
                                 qk_st[0][MROW:128, :, 1, b * T:b * T + S]).then_inc(done, 16)
                    sp.dma_start(qkc_st[par][MROW:128, :, 1, b * T + S:(b + 1) * T],
                                 qk_st[0][ZROW:ZROW + 2, :, 1, b * T + S:(b + 1) * T]).then_inc(done, 16)
            slots(sp, slot)

            def store(g, par):
                w(sp, "m_out_set", g + 1)
                src = m_out[par][:]
                at = bass.ds(g, 1) if not isinstance(g, int) else slice(g, g + 1)
                dst = out.rearrange("(g b) t c -> g t b c", b=MG)[at].rearrange("o t b c -> t (o b) c")
                sp.dma_start(dst, src).then_inc(sems[f"out{par}"], 16)

            with sp.Fori(0, NGRP // 2) as i:
                store(2 * i, 0)
                store(2 * i + 1, 1)
            w(sp, "out0", 16 * (NGRP // 2))
            w(sp, "out1", 16 * (NGRP // 2))

        @block.gpsimd
        def _(pool):
            nc.gpsimd.memset(ident[:], 0.0).then_inc(sems["z_pool"], 1)
            pool.wait_ge(sems["z_pool"], 1)
            nc.gpsimd.affine_select(out=ident[:], in_=ident[:], compare_op=ALU.not_equal, fill=1.0, base=0,
                                    pattern=[[-1, 128]], channel_multiplier=1).then_inc(sems["z_pool"], 1)
            pool.wait_ge(sems["z_pool"], 2)
            nc.gpsimd.tensor_copy(ident16[:], ident[:]).then_inc(sems["id_set"], 1)
            nc.gpsimd.memset(eps_sb[:], EPS).then_inc(sems["z_pool"], 1)
            nc.gpsimd.memset(mhalf[:], -0.5).then_inc(sems["z_pool"], 1)
            nc.gpsimd.memset(qk_st[0][:, :, 1].bitcast(u32), 0).then_inc(sems["z_pool"], 1)
            pool.wait_ge(sems["z_pool"], 5)
            nc.gpsimd.memset(qk_st[0][96:128, :, 1], 1.0).then_inc(sems["zk_set"], 1)
            pool.wait_ge(sems["zk_set"], 1)
            pool.wait_ge(sems["wq_in"], 16 * 3)
            for n, (src, at) in enumerate(((wqkv_sb, 0), (wqkv_sb, C), (wqc_sb, 0), (wkvc_sb, 0))):
                nc.gpsimd.tensor_copy(wdh[:, n].rearrange("c (d h) -> c d h", d=D),
                                      src[:, at:at + C].rearrange("c (h d) -> c d h", d=D)).then_inc(sems["wdh_set"], 1)

            def rstd(kind, p):
                L = ln[kind]
                w(pool, f"{kind}_mv_set", p.n + 1)
                nc.gpsimd.tensor_tensor(L["ve"][:], L["mv"][:, :, 1], eps_sb[0:L["rows"], 0:G],
                                        ALU.add).then_inc(sems[f"{kind}_ve_set"], 1)
                w(pool, f"{kind}_ve_set", p.n + 1)
                if not p.first():
                    w(pool, f"{kind}_n_set", p.n)
                nc.gpsimd.tensor_tensor(L["rstd"][:], L["ve"][:], mhalf[0:L["rows"], 0:G],
                                        ALU.pow).then_inc(sems[f"{kind}_rstd_set"], 1)

            def parts(p, rest, dst, left, mid, last, loaded):
                if not p.first():
                    q = p.shift(-1)
                    w(pool, f"{loaded}{q.par}", 16 * NCMB * (q.turn + 1))
                hold(pool, left, p.n + 1)
                nc.gpsimd.tensor_copy(dst[1], rest).then_inc(sems[mid], 1)
                w(pool, mid, p.n + 1)
                nc.gpsimd.tensor_tensor(dst[2], rest, dst[1], ALU.subtract).then_inc(sems[last], 1)

            def slot(s):
                a, h, d, f = (s.pair(n) for n in ("ahead", "here", "back1", "back2"))
                if a:
                    rstd("x", a)
                if f:
                    parts(f, qcr[:], [qkcp[:, 0, n] for n in range(3)], "qcr_set", "qc1_set", "qc2_set", "qkc_in")
                if a:
                    parts(a, qkr[:], [qkp[:, :, n] for n in range(3)], "qkr_set", "qk1_set", "qk2_set", "qk_in")
                if d:
                    rstd("x1", d)
                    parts(d, kcr[:].rearrange("c (b k) -> c b k", b=G), key_parts, "kcr_set", "kc1_set", "kc2_set", "qkc_in")
                if h:
                    rstd("ctx", h)

            slots(pool, slot)

            def m_rstd_step(g, first=False):
                w(pool, "m_mv_set", g + 1)
                nc.gpsimd.tensor_tensor(m_ve[:], m_mv[:, :, 1], eps_sb[:, 0:MG], ALU.add).then_inc(sems["m_ve_set"], 1)
                w(pool, "m_ve_set", g + 1)
                nc.gpsimd.tensor_tensor(m_rstd[:], m_ve[:], mhalf[:, 0:MG], ALU.pow).then_inc(sems["m_rstd_set"], 1)

            with pool.Fori(0, NGRP) as g:
                m_rstd_step(g)

        @block.vector
        def _(dve):
            nc.vector.memset(qk_st[0][:, :, 0].bitcast(u32), 0).then_inc(sems["zq_set"], 1)
            dve.wait_ge(sems["cond_t"], 1)
            nc.vector.tensor_copy(condT[:], ps_max[0][:, 0:B]).then_inc(sems["condT_set"], 1)
            dve.wait_ge(sems["tanh_set"], 1)
            nc.vector.tensor_scalar(tanh_c[:], tanh_c[:], 0.5, 0.5, ALU.mult, ALU.add).then_inc(sems["sig_set"], 1)
            dve.wait_ge(sems["sig_set"], 1)
            nc.vector.tensor_tensor(siluT[:], tanh_c[:], condT[:], ALU.mult).then_inc(sems["silu_set"], 1)

            def tables():
                dve.wait_ge(sems["mod_ps"], 1)
                dve.wait_ge(sems["b_in"], 16 * 41)
                for k in range(6):
                    last = nc.vector.tensor_scalar(mod[:, k], ps_max[0][:, k * B:(k + 1) * B], bmod_sb[:, k:k + 1],
                                                   1.0 if k in (1, 4) else 0.0, ALU.add, ALU.add)
                last.then_inc(sems["mod_set"], 1)

            def bias_tables():
                dve.wait_ge(sems["bo_ps"], 1)
                nc.vector.tensor_tensor(bo2[:], ps_max[1][:, 0:2], bo_sb[:, 0:2], ALU.add).then_inc(sems["bo_set"], 1)
                dve.wait_ge(sems["bo_set"], 1)
                dve.wait_ge(sems["mod_set"], 1)
                nc.vector.tensor_scalar(gb_a[:], mod[:, 2], bo2[:, 0:1], None, ALU.mult)
                nc.vector.tensor_scalar(gb_m[:], mod[:, 5], bo_sb[:, 2:3], None, ALU.mult).then_inc(sems["gb_set"], 1)

            def stats(kind, p, src):
                L = ln[kind]
                for b in range(G):
                    last = nc.vector.bn_stats(L["stats"][:, b], src(b))
                last.then_inc(sems[f"{kind}_stats_set"], 1)

            def aggregate(kind, p):
                L = ln[kind]
                hold(dve, f"{kind}_stats_set", p.n + 1)
                for b in range(G):
                    last = nc.vector.bn_aggr(L["mv"][:, b], L["stats"][:, b])
                last.then_inc(sems[f"{kind}_mv_set"], 1)

            def normalise(kind, p, src, taken):
                L = ln[kind]
                w(dve, f"{kind}_rstd_set", p.n + 1)
                if not p.first():
                    w(dve, taken, p.n)
                for b in range(G):
                    last = nc.vector.tensor_scalar(L["xn"][:, b], src(b), L["mv"][:, b, 0:1], L["rstd"][:, b:b + 1],
                                                   ALU.subtract, ALU.mult)
                last.then_inc(sems[f"{kind}_n_set"], 1)

            def arrived(name, p, rest_at):
                if p.first():
                    dve.wait_ge(sems[f"{name}0"], 16)
                elif isinstance(p.n, int) and p.n == rest_at:
                    for n in range(1, 4):
                        dve.wait_ge(sems[f"{name}{n}"], 16)

            def x_of(p):
                return lambda b: xs[:, batch(p, b)].rearrange("t o c -> t (o c)")

            def ctx_of(p):
                return lambda b: ctx_sb[:, batch(p, b)].rearrange("t o c -> t (o c)")

            def maxima(p, u, s, stream, ready, mxt, keys, done):
                b, c = divmod(u, 4)
                bank, _ = s.bank_before(MAX_RING, stream, u)
                w(dve, ready, NU * p.n + u + 1)
                src = ps_max[bank][:, :].rearrange("q (j k) -> q j k", j=4)[:, :, 0:keys]
                nc.vector.reduce_max(mxt[:, b].rearrange("q (j i) -> q j i", i=4)[:, :, c], src,
                                     AX.X).then_inc(sems[done], 1)

            def minus_max(p, b, mxt, nmt, counted, high, both, taken):
                w(dve, counted, NU * p.n + 4 * b + 4)
                if not p.first():
                    w(dve, taken, 2 * p.n + b - 1)
                nc.vector.tensor_scalar(nmt[:, b, 0], mxt[:, b], -1.0, None, ALU.mult).then_inc(sems[high], 1)
                w(dve, high, 2 * p.n + b + 1)
                nc.vector.scalar_tensor_tensor(nmt[:, b, 1], mxt[:, b], -1.0, nmt[:, b, 0], ALU.mult,
                                               ALU.subtract).then_inc(sems[both], 1)

            def empty_max(p, b, job, ready, dst, name, loaded):
                w(dve, ready, 2 * p.n + b + 1)
                if not p.first():
                    q = p.shift(-1)
                    w(dve, f"{loaded}{q.par}", 16 * G * (q.turn + 1))
                nc.vector.tensor_copy(dst[:, b], ps_misc[BANK[job]][:].bitcast(bf16)[0:2 * H, 0:T]).then_inc(sems[name], 1)

            def attention_out(p, kind, job, ready, rden_name, name, taken):
                src = ps_misc[BANK[job]][:].rearrange("q (r m x) -> q r m x", r=2 * G, x=2 * D)
                w(dve, ready, p.n + 1)
                nc.vector.reciprocal(att[kind]["rden"][:], src[:, :, :, D]).then_inc(sems[rden_name], 1)
                if not p.first():
                    w(dve, taken, p.n)
                w(dve, rden_name, p.n + 1)
                nc.vector.tensor_tensor(att[kind]["o"][:], src[:, :, :, 0:D],
                                        att[kind]["rden"][:].unsqueeze(3).to_broadcast([T, 2 * G, 8, D]),
                                        ALU.mult).then_inc(sems[name], 1)

            def rest(psum, bias, part, dst):
                return nc.vector.scalar_tensor_tensor(dst, psum, bias, part, ALU.add, ALU.subtract)

            def residual(p, ready, job, name):
                w(dve, ready, p.n + 1)
                nc.vector.tensor_tensor(xs[:, batches(p)], xs[:, batches(p)],
                                        ps_misc[BANK[job]][:, 0:GT].rearrange("t (b c) -> t b c", b=G),
                                        ALU.add).then_inc(sems[name], 1)

            def zeros():
                nc.vector.memset(qkcp[:].bitcast(u32), 0).then_inc(sems["pad_set"], 1)
                for vt in (*v_m, *vc_m):
                    last = nc.vector.memset(vt[:], 0.0)
                last.then_inc(sems["z_dve"], 1)
                dve.wait_ge(sems["z_dve"], 1)
                for vt, keys in ((v_m[0], T), (v_m[1], T), (vc_m[0], S), (vc_m[1], S)):
                    for s_ in range(2):
                        last = nc.vector.memset(vt[0:keys].rearrange("t b (m s) n -> t (b m) s n", s=2)[
                            :, :, s_, 2 * D * s_ + D:2 * D * s_ + D + 1], 1.0)
                last.then_inc(sems["zv_set"], 1)

            def slot(s):
                a, h, d, f, e = (s.pair(n) for n in ("ahead", "here", "back1", "back2", "back3"))
                for t in range(TICKS):
                    if t == 0 and e:
                        minus_max(e, 1, mxc, nmc, "mxc_set", "nmch_set", "nmc_set", "mtc_ps")
                    if t == 1 and e:
                        empty_max(e, 1, "max_c1", "mtc_ps", nmcT, "nmcT_set", "mc_in")
                    if t == 3 and d:
                        attention_out(d, "s", "o_t", "ot_ps", "rden_set", "o_set", "obt_ps")
                    if t == 4 and h:
                        minus_max(h, 0, mx, nm, "mx_set", "nmh_set", "nm_set", "mts_ps")
                    if t == 5 and h:
                        empty_max(h, 0, "max_s0", "mts_ps", nmT, "nmT_set", "m_in")
                    if t == 8 and h:
                        minus_max(h, 1, mx, nm, "mx_set", "nmh_set", "nm_set", "mts_ps")
                    if t == 9 and h:
                        empty_max(h, 1, "max_s1", "mts_ps", nmT, "nmT_set", "m_in")
                    if t == 10 and e:
                        attention_out(e, "c", "oc_t", "oct_ps", "rdenc_set", "oc_set", "obct_ps")
                    if t == 11 and d:
                        normalise("x1", d, x_of(d), "x1t_ps")
                    if t == 12 and f:
                        minus_max(f, 0, mxc, nmc, "mxc_set", "nmch_set", "nmc_set", "mtc_ps")
                    if t == 13 and f:
                        empty_max(f, 0, "max_c0", "mtc_ps", nmcT, "nmcT_set", "mc_in")

                    use = s.unit(self_max(t))
                    if use:
                        maxima(*use, s, "self", "smax_ps", mx, T, "mx_set")
                    use = s.unit(cross_max(t))
                    if use:
                        maxima(*use, s, "cross", "smaxc_ps", mxc, S, "mxc_set")

                    if t == 0 and a:
                        arrived("x_in", a, 2 * LOOP[0])
                        stats("x", a, x_of(a))
                        aggregate("x", a)
                    if t == 2 and a:
                        normalise("x", a, x_of(a), "xt_ps")
                        if a.first():
                            tables()
                            zeros()
                    if t == 6 and a:
                        w(dve, "qk0_set", a.n + 1)
                        if not a.first():
                            w(dve, "qk2_set", a.n)
                        rest(ps_misc[BANK["qk"]][:, 0:GT], bdh[:, 0:1], qkp[:, 0, 0], qkr[:, 0])
                        rest(ps_misc[BANK["qk"]][:, GT:2 * GT], bdh[:, 1:2], qkp[:, 1, 0],
                             qkr[:, 1]).then_inc(sems["qkr_set"], 1)
                    if t == 8 and d:
                        residual(d, "yt_ps", "y_t", "x1_set")
                        hold(dve, "x1_set", d.n + 1)
                        stats("x1", d, x_of(d))
                        aggregate("x1", d)
                    if t == 10 and d:
                        w(dve, "kvc0_set", d.n + 1)
                        if not d.first():
                            w(dve, "kc2_set", d.n)
                        rest(ps_misc[BANK["kv_c"]][:, 0:GS].rearrange("c (b k) -> c b k", b=G), bdh[:, 3:4],
                             key_parts[0], kcr[:].rearrange("c (b k) -> c b k", b=G)).then_inc(sems["kcr_set"], 1)
                    if t == 13 and h:
                        arrived("c_in", h, 2 * LOOP[0] - 1)
                        stats("ctx", h, ctx_of(h))
                        aggregate("ctx", h)
                    if t == 15:
                        if h:
                            normalise("ctx", h, ctx_of(h), "ctxt_ps")
                        if e:
                            residual(e, "yct_ps", "yc_t", "x2_set")
                        if d:
                            w(dve, "qc0_set", d.n + 1)
                            if not d.first():
                                w(dve, "qc2_set", d.n)
                            rest(ps_misc[BANK["q_c"]][:, 0:GT], bdh[:, 2:3], qkcp[:, 0, 0], qcr[:]).then_inc(sems["qcr_set"], 1)
                if a and a.first():
                    bias_tables()

            slots(dve, slot)

            def group(g):
                return bass.ds(MG * g, MG) if not isinstance(g, int) else slice(MG * g, MG * g + MG)

            def one(g, b):
                at = bass.ds(MG * g + b, 1) if not isinstance(g, int) else slice(MG * g + b, MG * g + b + 1)
                return xs[:, at].rearrange("t o c -> t (o c)")

            def m_norm(g, par, first=False):
                if not first:
                    hold(dve, "m_n_set", g)
                for b in range(MG):
                    last = nc.vector.bn_stats(m_stats[:, b], one(g, b))
                last.then_inc(sems["m_stats_set"], 1)
                hold(dve, "m_stats_set", g + 1)
                for b in range(MG):
                    last = nc.vector.bn_aggr(m_mv[:, b], m_stats[:, b])
                last.then_inc(sems["m_mv_set"], 1)
                if not first and not (isinstance(g, int) and g < 2):
                    hold(dve, "m_nt_ps", g - 1)
                w(dve, "m_rstd_set", g + 1)
                for b in range(MG):
                    last = nc.vector.tensor_scalar(m_n[par][:, b], one(g, b), m_mv[:, b, 0:1], m_rstd[:, b:b + 1],
                                                   ALU.subtract, ALU.mult)
                last.then_inc(sems["m_n_set"], 1)

            def m_residual(g, par, first=False):
                w(dve, "m_yt_ps", g + 1)
                if not first:
                    w(dve, f"out{par}", 16 * (g // 2) if isinstance(g, int) else 8 * (g - par))
                nc.vector.tensor_tensor(m_out[par][:], xs[:, group(g)],
                                        ps[7][:, :].rearrange("t (b c) -> t b c", b=MG), ALU.add).then_inc(sems["m_out_set"], 1)

            dve.wait_ge(sems["x2_set"], NPAIR)
            m_norm(0, 0, True)
            m_norm(1, 1)
            m_norm(2, 0)
            m_residual(0, 0, True)
            m_norm(3, 1)
            m_residual(1, 1, True)
            with dve.Fori(1, NGRP // 2 - 1) as i:
                m_norm(2 * i + 2, 0)
                m_residual(2 * i, 0)
                m_norm(2 * i + 3, 1)
                m_residual(2 * i + 1, 1)
            m_residual(NGRP - 2, 0)
            m_residual(NGRP - 1, 1)

        @block.scalar
        def _(act):
            act.wait_ge(sems["condT_set"], 1)
            nc.scalar.activation(tanh_c[:], condT[:], ACT.Tanh, scale=0.5).then_inc(sems["tanh_set"], 1)

            def exps(p, u, s, stream, ready, dst, name, pv):
                bank, _ = s.bank_before(EXP_RING, stream, u)
                w(act, ready, NU * p.n + u + 1)
                if u >= 2 or not p.first():
                    w(act, pv, NU * p.n + u - 1)
                nc.scalar.activation(dst[u % 2][:].rearrange("k j q -> k (j q)"), ps_st[bank][:, :],
                                     ACT.Exp, scale=SCALE).then_inc(sems[name], 1)

            def values(dst, keys, src):
                for s_ in range(2):
                    for b in range(G):
                        last = nc.scalar.activation(
                            dst[0:keys, b].rearrange("t (m s) n -> t m s n", s=2)[:, :, s_, 2 * D * s_:2 * D * s_ + D],
                            src[:, b * C:(b + 1) * C].rearrange("t (m s d) -> t m s d", s=2, d=D)[:, :, s_, :], ACT.Copy)
                return last

            def sums(p, kind, src, ready, name, taken):
                w(act, ready, NU * p.n + NU)
                if not p.first():
                    w(act, taken, p.n)
                nc.scalar.activation(att[kind]["sum"][:].rearrange("c b r q -> c (b r q)"), src[:, :],
                                     ACT.Copy).then_inc(sems[name], 1)

            def copy(dst, src, ready, p, name, taken):
                w(act, ready, p.n + 1)
                if not p.first():
                    w(act, taken, p.n)
                nc.scalar.activation(dst, src, ACT.Copy).then_inc(sems[name], 1)

            def slot(s):
                a, h, d, f, e = (s.pair(n) for n in ("ahead", "here", "back1", "back2", "back3"))
                for t in range(TICKS):
                    if t == 1 and d:
                        sums(d, "s", ps_o, "pv_ps", "sum_set", "ot_ps")
                    if t == 2 and d:
                        copy(cT[:], ps_misc[BANK["ctx_t"]][:, 0:GS], "ctxt_ps", d, "cT_set", "kvc_ps")
                    if t == 4 and a:
                        w(act, "xt_ps", a.n + 1)
                        if a.first():
                            act.wait_ge(sems["mod_set"], 1)
                        else:
                            w(act, "v_ps", a.n)
                        for b in range(G):
                            last = nc.scalar.activation(xmT[:, b * T:(b + 1) * T],
                                                        ps_misc[BANK["x_t"]][:, b * T:(b + 1) * T], ACT.Identity,
                                                        bias=column(mod[:, 0], a, b), scale=column(mod[:, 1], a, b))
                        last.then_inc(sems["xmT_set"], 1)
                    if t == 5 and d:
                        copy(oT[:], ps_misc[BANK["ob_t"]][:, 0:GT], "obt_ps", d, "oT_set", "proj_ps")
                    if t == 6 and a:
                        w(act, "qk_ps", a.n + 1)
                        src = ps_misc[BANK["qk"]]
                        if a.first():
                            act.wait_ge(sems["b_in"], 16 * 41)
                        else:
                            q = a.shift(-1)
                            w(act, f"qk_in{q.par}", 16 * NCMB * (q.turn + 1))
                        nc.scalar.activation(qkp[:, 0, 0], src[:, 0:GT], ACT.Identity, bias=bdh[:, 0:1])
                        nc.scalar.activation(qkp[:, 1, 0], src[:, GT:2 * GT], ACT.Identity,
                                             bias=bdh[:, 1:2]).then_inc(sems["qk0_set"], 1)
                    if t == 7 and d:
                        w(act, "proj_ps", d.n + 1)
                        if not d.first():
                            w(act, "yt_ps", d.n)
                        for b in range(G):
                            last = nc.scalar.activation(yT[:, b * T:(b + 1) * T],
                                                        ps_misc[BANK["proj"]][:, b * T:(b + 1) * T], ACT.Identity,
                                                        bias=column(gb_a, d, b), scale=column(mod[:, 2], d, b))
                        last.then_inc(sems["y_set"], 1)
                    if t == 9 and e:
                        sums(e, "c", ps_oc, "pvc_ps", "sumc_set", "oct_ps")
                    if t == 10 and d:
                        w(act, "kvc_ps", d.n + 1)
                        src = ps_misc[BANK["kv_c"]]
                        if d.first():
                            act.wait_ge(sems["pad_set"], 1)
                        else:
                            q = d.shift(-1)
                            w(act, f"qkc_in{q.par}", 16 * NCMB * (q.turn + 1))
                        nc.scalar.activation(key_parts[0], src[:, 0:GS].rearrange("c (b k) -> c b k", b=G), ACT.Identity,
                                             bias=bdh[:, 3:4])
                        if not d.first(2):
                            w(act, "pvc_ps", NU * (d.n - 1))
                        values(vc_m[d.par], S, src[0:S, GS:GS + G * C]).then_inc(sems["kvc0_set"], 1)
                    if t == 11 and a:
                        w(act, "v_ps", a.n + 1)
                        if a.first():
                            act.wait_ge(sems["zv_set"], 1)
                        if not a.first(2):
                            w(act, "pv_ps", NU * (a.n - 1))
                        values(v_m[a.par], T, ps_misc[BANK["v"]][:, 0:G * C]).then_inc(sems["v_set"], 1)
                    if t == 12:
                        if e:
                            copy(ocT[:], ps_misc[BANK["obc_t"]][:, 0:GT], "obct_ps", e, "ocT_set", "projc_ps")
                        if d:
                            w(act, "x1t_ps", d.n + 1)
                            nc.scalar.activation(x1T[:], ps_misc[BANK["x1_t"]][:, 0:GT], ACT.Copy).then_inc(sems["x1T_set"], 1)
                    if t == 14 and e:
                        w(act, "projc_ps", e.n + 1)
                        if not e.first():
                            w(act, "yct_ps", e.n)
                        nc.scalar.activation(ycT[:], ps_misc[BANK["proj_c"]][:, 0:GT], ACT.Identity,
                                             bias=bo2[:, 1:2]).then_inc(sems["yc_set"], 1)
                    if t == 15 and d:
                        w(act, "qc_ps", d.n + 1)
                        if not d.first():
                            q = d.shift(-1)
                            w(act, f"qkc_in{q.par}", 16 * NCMB * (q.turn + 1))
                        nc.scalar.activation(qkcp[:, 0, 0], ps_misc[BANK["q_c"]][:, 0:GT], ACT.Identity,
                                             bias=bdh[:, 2:3]).then_inc(sems["qc0_set"], 1)

                    use = s.unit(self_exp(t))
                    if use:
                        exps(*use, s, "self", "st_ps", p_s, "exp_set", "pv_ps")
                    use = s.unit(cross_exp(t))
                    if use:
                        exps(*use, s, "cross", "stc_ps", p_c, "expc_set", "pvc_ps")

            slots(act, slot)

            def one(tile, g, b):
                return tile[:, bass.ds(MG * g + b, 1) if not isinstance(g, int) else slice(MG * g + b, MG * g + b + 1)]

            def m_modulate(g, par, first=False):
                w(act, "m_nt_ps", g + 1)
                for b in range(MG):
                    last = nc.scalar.activation(m_nT[par][:, b * T:(b + 1) * T], ps[0][:, b * T:(b + 1) * T], ACT.Identity,
                                                bias=one(mod[:, 3], g, b), scale=one(mod[:, 4], g, b))
                last.then_inc(sems["m_nT_set"], 1)

            def m_gelu(g, par, first=False):
                for k in range(NF):
                    w(act, "m_h_ps", NF * g + k + 1)
                    nc.scalar.activation(hT[par][:, k], ps[2 + k][:, :], ACT.Gelu_apprx_tanh,
                                         bias=b1_sb[:, k:k + 1]).then_inc(sems["m_hT_set"], 1)

            def m_gate(g, par, first=False):
                w(act, "m_y_ps", g + 1)
                for b in range(MG):
                    last = nc.scalar.activation(m_y[par][:, b * T:(b + 1) * T], ps[6][:, b * T:(b + 1) * T], ACT.Identity,
                                                bias=one(gb_m, g, b), scale=one(mod[:, 5], g, b))
                last.then_inc(sems["m_y_set"], 1)

            m_modulate(0, 0, True)
            with act.Fori(0, NGRP // 2 - 1) as i:
                for k in range(2):
                    m_gelu(2 * i + k, k)
                    m_modulate(2 * i + k + 1, (k + 1) % 2)
                    m_gate(2 * i + k, k)
            m_gelu(NGRP - 2, 0)
            m_modulate(NGRP - 1, 1)
            m_gate(NGRP - 2, 0)
            m_gelu(NGRP - 1, 1)
            m_gate(NGRP - 1, 1)

        @block.tensor
        def _(pe):
            mm, tr = nc.tensor.matmul, nc.tensor.transpose

            pe.wait_ge(sems["id_set"], 1)
            pe.wait_ge(sems["wm_in"], 16 * 2)
            tr(ps_max[0][:, 0:B], cond_sb[:], ident[0:B, 0:B]).then_inc(sems["cond_t"], 1)
            pe.wait_ge(sems["silu_set"], 1)
            for k in range(6):
                last = mm(ps_max[0][:, k * B:(k + 1) * B], wmod_sb[:, k * C:(k + 1) * C], siluT[:], start=True, stop=True)
            last.then_inc(sems["mod_ps"], 1)

            def bank(s, name):
                before = s.job_before(name)
                if before:
                    job, p = before
                    name_, count = EMPTIED[job]
                    w(pe, name_, count(p))
                return ps_misc[BANK[name]]

            def scores(p, u, dst, st, keys, counted):
                b, c = divmod(u, 4)
                for j in range(4):
                    h = 4 * j + c
                    last = mm(dst[:, j * T:j * T + keys], st[p.par][0:MROW, h, 0, b * T:(b + 1) * T],
                              st[p.par][0:MROW, h, 1, b * T:b * T + keys], start=True, stop=True)
                last.then_inc(sems[counted], 1)

            def scores_t(p, u, dst, st, counted):
                b, c = divmod(u, 4)
                for j in range(4):
                    h = 4 * j + c
                    last = mm(dst[:, j * T:(j + 1) * T], st[p.par][:, h, 1, b * T:(b + 1) * T],
                              st[p.par][:, h, 0, b * T:(b + 1) * T], start=True, stop=True)
                last.then_inc(sems[counted], 1)

            def values(p, u, probs, dst, vt, counted):
                b, c = divmod(u, 4)
                r, s_ = divmod(c, 2)
                at = (b * 2 + r) * T
                for j in range(4):
                    last = mm(dst[32 * j:32 * j + 32, at:at + T], vt[p.par][:, b, 4 * j + c], probs[u % 2][:, j],
                              start=(s_ == 0), stop=(s_ == 1))
                last.then_inc(sems[counted], 1)

            def ring_bank(s, uses, tiles, stream, u, names):
                n, before = s.bank_before(uses, stream, u)
                if before:
                    name, q, unit = before
                    w(pe, names[name], NU * q.n + unit + 1)
                return tiles[n]

            def slot(s):
                a, h, d, f, e = (s.pair(n) for n in ("ahead", "here", "back1", "back2", "back3"))
                max_read = {"self": "mx_set", "cross": "mxc_set"}
                exp_read = {"self": "exp_set", "cross": "expc_set"}

                def transposed(job, kind, p, rows, counted):
                    dst = bank(s, job)
                    w(pe, f"{kind}_n_set", p.n + 1)
                    for b in range(G):
                        last = tr(dst[:, b * rows:(b + 1) * rows], ln[kind]["xn"][:, b], ident[0:rows, 0:rows])
                    last.then_inc(sems[counted], 1)

                def flip(job, p, srcs, ready, counted):
                    dst = bank(s, job)
                    w(pe, ready, p.n + 1)
                    for n, src in enumerate(srcs):
                        last = tr(dst[:, n * 128:(n + 1) * 128], src, ident[:])
                    last.then_inc(sems[counted], 1)

                def flip_sums(job, kind, p, ready, counted):
                    flip(job, p, [att[kind]["sum"][:, b, r] for b in range(G) for r in range(2)], ready, counted)

                def flip_out(job, kind, p, ready, counted):
                    flip(job, p, [att[kind]["o"][:, 2 * b:2 * b + 2].rearrange("q r m d -> q (r m d)") for b in range(G)],
                         ready, counted)

                def flip_y(job, src, p, ready, counted):
                    flip(job, p, [src[:, b * T:(b + 1) * T] for b in range(G)], ready, counted)

                def project(job, p, weights, src, ready, counted, cols=GT):
                    dst = bank(s, job)
                    w(pe, ready, p.n + 1)
                    mm(dst[:, 0:cols], weights, src, start=True, stop=True).then_inc(sems[counted], 1)

                def max_t(job, p, b, src, ready, counted):
                    dst = bank(s, job)
                    w(pe, ready, 2 * p.n + b + 1)
                    tr(dst[:].bitcast(bf16)[0:2 * H, 0:T], src[:, b].rearrange("q r h -> q (r h)"),
                       ident16[:]).then_inc(sems[counted], 1)

                for t in range(TICKS):
                    use = s.unit(self_max(t))
                    if use:
                        p, u = use
                        dst = ring_bank(s, MAX_RING, ps_max, "self", u, max_read)
                        if u == 0:
                            w(pe, f"qk_in{p.par}", 16 * NCMB * (p.turn + 1))
                        scores(p, u, dst, qk_st, T, "smax_ps")
                    use = s.unit(cross_max(t))
                    if use:
                        p, u = use
                        dst = ring_bank(s, MAX_RING, ps_max, "cross", u, max_read)
                        if u == 0:
                            w(pe, f"qkc_in{p.par}", 16 * NCMB * (p.turn + 1))
                        scores(p, u, dst, qkc_st, S, "smaxc_ps")
                    use = s.unit(self_exp(t))
                    if use:
                        p, u = use
                        dst = ring_bank(s, EXP_RING, ps_st, "self", u, exp_read)
                        if u % 4 == 0:
                            w(pe, f"m_in{p.par}", 16 * (G * p.turn + u // 4 + 1))
                        scores_t(p, u, dst, qk_st, "st_ps")
                    use = s.unit(cross_exp(t))
                    if use:
                        p, u = use
                        dst = ring_bank(s, EXP_RING, ps_st, "cross", u, exp_read)
                        if u % 4 == 0:
                            w(pe, f"mc_in{p.par}", 16 * (G * p.turn + u // 4 + 1))
                        scores_t(p, u, dst, qkc_st, "stc_ps")
                    use = s.unit(self_pv(t))
                    if use:
                        p, u = use
                        w(pe, "exp_set", NU * p.n + u + 1)
                        if u == 0:
                            w(pe, "v_set", p.n + 1)
                            if not p.first():
                                w(pe, "sum_set", p.n)
                        values(p, u, p_s, ps_o, v_m, "pv_ps")
                    use = s.unit(cross_pv(t))
                    if use:
                        p, u = use
                        w(pe, "expc_set", NU * p.n + u + 1)
                        if u == 0 and not p.first():
                            w(pe, "sumc_set", p.n)
                        values(p, u, p_c, ps_oc, vc_m, "pvc_ps")

                    if t == 0 and e:
                        max_t("max_c1", e, 1, nmc, "nmc_set", "mtc_ps")
                    if t == 1 and d:
                        transposed("ctx_t", "ctx", d, S, "ctxt_ps")
                    if t == 2 and d:
                        flip_sums("o_t", "s", d, "sum_set", "ot_ps")
                    if t == 3 and a:
                        transposed("x_t", "x", a, T, "xt_ps")
                    if t == 4:
                        if d:
                            flip_out("ob_t", "s", d, "o_set", "obt_ps")
                        if h:
                            max_t("max_s0", h, 0, nm, "nm_set", "mts_ps")
                    if t == 5 and a:
                        dst = bank(s, "qk")
                        if a.first():
                            pe.wait_ge(sems["wdh_set"], 4)
                        w(pe, "xmT_set", a.n + 1)
                        mm(dst[:, 0:GT], wdh[:, 0], xmT[:], start=True, stop=True)
                        mm(dst[:, GT:2 * GT], wdh[:, 1], xmT[:], start=True, stop=True).then_inc(sems["qk_ps"], 1)
                    if t == 6 and d:
                        project("proj", d, wproj_sb[:], oT[:], "oT_set", "proj_ps")
                    if t == 7 and d:
                        flip_y("y_t", yT, d, "y_set", "yt_ps")
                    if t == 8 and h:
                        max_t("max_s1", h, 1, nm, "nm_set", "mts_ps")
                    if t == 9:
                        if d:
                            dst = bank(s, "kv_c")
                            w(pe, "cT_set", d.n + 1)
                            mm(dst[:, 0:GS], wdh[:, 3], cT[:], start=True, stop=True)
                            for b in range(G):
                                last = mm(dst[0:S, GS + b * C:GS + (b + 1) * C], cT[:, b * S:(b + 1) * S],
                                          wkvc_sb[:, C:2 * C], start=True, stop=True)
                            last.then_inc(sems["kvc_ps"], 1)
                        if e:
                            flip_sums("oc_t", "c", e, "sumc_set", "oct_ps")
                    if t == 10 and a:
                        dst = bank(s, "v")
                        for b in range(G):
                            last = mm(dst[:, b * C:(b + 1) * C], xmT[:, b * T:(b + 1) * T], wqkv_sb[:, 2 * C:3 * C],
                                      start=True, stop=True)
                        last.then_inc(sems["v_ps"], 1)
                    if t == 11:
                        if e:
                            flip_out("obc_t", "c", e, "oc_set", "obct_ps")
                        if d:
                            transposed("x1_t", "x1", d, T, "x1t_ps")
                    if t == 12 and f:
                        max_t("max_c0", f, 0, nmc, "nmc_set", "mtc_ps")
                    if t == 13 and e:
                        project("proj_c", e, wcproj_sb[:], ocT[:], "ocT_set", "projc_ps")
                    if t == 14:
                        if d:
                            project("q_c", d, wdh[:, 2], x1T[:], "x1T_set", "qc_ps")
                        if e:
                            flip_y("yc_t", ycT, e, "yc_set", "yct_ps")
                if a and a.first():
                    pe.wait_ge(sems["w_in"], 16 * 6)
                    pe.wait_ge(sems["b_in"], 16 * 41)
                    mm(ps_max[1][:, 0:1], wproj_sb[:], bv_sb[:, 0:1], start=True, stop=True)
                    mm(ps_max[1][:, 1:2], wcproj_sb[:], bv_sb[:, 1:2], start=True, stop=True).then_inc(sems["bo_ps"], 1)
                    pe.wait_ge(sems["gb_set"], 1)

            slots(pe, slot)

            def m_transpose(g, par, first=False):
                w(pe, "m_n_set", g + 1)
                if not first:
                    w(pe, "m_nT_set", g)
                for b in range(MG):
                    last = tr(ps[0][:, b * T:(b + 1) * T], m_n[par][:, b], ident[:])
                last.then_inc(sems["m_nt_ps"], 1)

            def m_up(g, par, first=False):
                w(pe, "m_nT_set", g + 1)
                for k in range(NF):
                    if not first:
                        w(pe, "m_hT_set", NF * g - NF + k + 1)
                    mm(ps[2 + k][:, :], w1_sb[:, k * 128:(k + 1) * 128], m_nT[par][:], start=True,
                       stop=True).then_inc(sems["m_h_ps"], 1)

            def m_down(g, par, first=False):
                if not first:
                    w(pe, "m_y_set", g)
                for k in range(NF):
                    w(pe, "m_hT_set", NF * g + k + 1)
                    last = mm(ps[6][:, :], w2_sb[:, k], hT[par][:, k], start=(k == 0), stop=(k == NF - 1))
                last.then_inc(sems["m_y_ps"], 1)

            def m_back(g, par, first=False):
                w(pe, "m_y_set", g + 1)
                if not first:
                    w(pe, "m_out_set", g)
                for b in range(MG):
                    last = tr(ps[7][:, b * C:(b + 1) * C], m_y[par][:, b * T:(b + 1) * T], ident[:])
                last.then_inc(sems["m_yt_ps"], 1)

            pe.wait_ge(sems["x2_set"], NPAIR)
            m_transpose(0, 0, True)
            m_up(0, 0, True)
            m_transpose(1, 1)
            m_down(0, 0, True)
            m_up(1, 1)
            m_back(0, 0, True)
            m_transpose(2, 0)
            m_down(1, 1)
            with pe.Fori(1, NGRP // 2 - 1) as i:
                for k in range(2):
                    m_up(2 * i + k, k)
                    m_back(2 * i + k - 1, (k + 1) % 2)
                    m_transpose(2 * i + k + 1, (k + 1) % 2)
                    m_down(2 * i + k, k)
            m_up(NGRP - 2, 0)
            m_back(NGRP - 3, 1)
            m_transpose(NGRP - 1, 1)
            m_down(NGRP - 2, 0)
            m_up(NGRP - 1, 1)
            m_back(NGRP - 2, 0)
            m_down(NGRP - 1, 1)
            m_back(NGRP - 1, 1)


_INS = ["x", "cond_1024", "ctx_1024"] + ["L0_xcond_" + n for n in (
    "W_mod", "b_mod", "W_qkv", "b_qkv", "W_proj", "b_proj", "W_qc", "b_qc", "W_kvc", "b_kvc", "W_cproj", "b_cproj",
    "W_mlp1", "b_mlp1", "W_mlp2", "b_mlp2")]


def kernel(**inputs):
    import numpy as np
    import concourse.bacc as bacc
    from concourse.bass_utils import run_bass_kernel_spmd

    nc = bacc.Bacc("TRN2", target_bir_lowering=False, num_devices=1)
    arrays, args = {}, []
    for name in _INS:
        a = np.ascontiguousarray(inputs[name])
        arrays[name] = a
        args.append(nc.dram_tensor(name, a.shape, mybir.dt.from_np(a.dtype), kind="ExternalInput").ap())
    args.append(nc.dram_tensor("out", (B, T, C), mybir.dt.float32, kind="ExternalOutput").ap())
    block_kernel(nc, *args)
    r = run_bass_kernel_spmd(nc, [arrays], core_ids=[0])
    return r.results[0]["out"]
```

```python
from contextlib import ExitStack

import concourse.bass as bass
from concourse import mybir

B, T, C = 32, 128, 128
H, D = 16, 8
S = 77
F = 512
G = 2
NPAIR = B // G
GT, GS = G * T, G * S
NF = F // 128
MG = 4
NGRP = B // MG
NU = 8
TICKS = 2 * NU
EPS = 1e-6
SCALE = float(D) ** -0.5
COMBOS = [(0, 0), (0, 1), (1, 0), (1, 1), (0, 2), (2, 0)]
NCMB = len(COMBOS)
ZROW = D * NCMB
MROW = 126


def self_max(t):
    return ("here", t) if t < NU else None


def self_exp(t):
    return ("here", t - NU) if t >= NU else None


def self_pv(t):
    return ("here", t - NU - 1) if t > NU else ("back1", NU - 1) if t == 0 else None


def cross_max(t):
    return ("back2", t - NU) if t >= NU else None


def cross_exp(t):
    return ("back3", t) if t < NU else None


def cross_pv(t):
    return ("back3", t - 1) if 1 <= t <= NU else None


def ring(*streams):
    return [(n, *f(t)) for t in range(TICKS) for n, f in streams if f(t)]


MAX_RING = ring(("self", self_max), ("cross", cross_max))
EXP_RING = ring(("self", self_exp), ("cross", cross_exp))

MISC = [("max_c1", "back3", 0), ("o_t", "back1", 1), ("ctx_t", "back1", 0), ("x_t", "ahead", 0),
        ("ob_t", "back1", 1), ("max_s0", "here", 0), ("qk", "ahead", 1), ("proj", "back1", 0), ("v", "ahead", 1),
        ("y_t", "back1", 0), ("max_s1", "here", 1), ("oc_t", "back3", 1), ("kv_c", "back1", 0), ("obc_t", "back3", 1),
        ("max_c0", "back2", 0), ("x1_t", "back1", 1), ("proj_c", "back3", 0), ("q_c", "back1", 1)]
BANK = {name: bank for name, _, bank in MISC}


class Pair:

    def __init__(self, i, k):
        self.i, self.k = i, k
        self.n = 2 * i + k
        self.par = k % 2
        self.turn = i + k // 2

    def exists(self):
        return not isinstance(self.n, int) or 0 <= self.n < NPAIR

    def first(self, m=1):
        return isinstance(self.n, int) and self.n < m

    def shift(self, d):
        return Pair(self.i, self.k + d)


class Slot:
    def __init__(self, i, k):
        here = Pair(i, k)
        self.pairs = {"far": here.shift(2), "ahead": here.shift(1), "here": here,
                      "back1": here.shift(-1), "back2": here.shift(-2), "back3": here.shift(-3)}
        self.i, self.k = i, k

    def pair(self, whose):
        p = self.pairs[whose]
        return p if p.exists() else None

    def unit(self, use):
        return (self.pair(use[0]), use[1]) if use and self.pair(use[0]) else None

    def last(self, n=0):
        return isinstance(self.i, int) and 2 * self.i + self.k == LAST_SLOT - n

    def before(self):
        return Slot(self.i, self.k - 1)

    def bank_before(self, uses, stream, u):
        at = next(n for n, (name, _, unit) in enumerate(uses) if (name, unit) == (stream, u))
        bank, slot = at % 2, self
        for _ in range(3 * len(uses)):
            at -= 2
            if at < 0:
                slot, at = slot.before(), at + len(uses)
            name, whose, unit = uses[at]
            if slot.pairs[whose].exists():
                return bank, (name, slot.pairs[whose], unit)
        return bank, None

    def job_before(self, name):
        names = [m[0] for m in MISC]
        slot, at = self, names.index(name)
        for _ in range(4 * len(MISC)):
            at -= 1
            if at < 0:
                slot, at = slot.before(), len(MISC) - 1
            job, whose, bank = MISC[at]
            if bank == BANK[name] and slot.pairs[whose].exists():
                return job, slot.pairs[whose]
        return None


FIRST_SLOT, LAST_SLOT = -2, NPAIR + 2
LOOP = (2, (NPAIR - 2) // 2)


def slots(engine, emit):
    for s in range(FIRST_SLOT, 2 * LOOP[0]):
        emit(Slot(s // 2, s % 2))
    with engine.Fori(LOOP[0], LOOP[1]) as i:
        emit(Slot(i, 0))
        emit(Slot(i, 1))
    for s in range(2 * LOOP[1], LAST_SLOT + 1):
        emit(Slot(s // 2, s % 2))


def block_kernel(nc, x, cond, ctx, w_mod, b_mod, w_qkv, b_qkv, w_proj, b_proj, w_qc, b_qc, w_kvc, b_kvc,
                 w_cproj, b_cproj, w_mlp1, b_mlp1, w_mlp2, b_mlp2, out):
    f32, bf16 = mybir.dt.float32, mybir.dt.bfloat16
    ALU, ACT, AX = mybir.AluOpType, mybir.ActivationFunctionType, mybir.AxisListType

    es = ExitStack()
    with es:
        def sb(name, shape, dt=f32):
            return es.enter_context(nc.sbuf_tensor(name, shape, dt))

        def pairbuf(name, shape, dt=f32):
            return [sb(f"{name}{i}", shape, dt) for i in range(2)]

        sems = {}

        def sem(name):
            sems[name] = es.enter_context(nc.semaphore(name))
            return sems[name]

        xs = sb("xs", [T, B, C])
        ctx_sb = sb("ctx_sb", [S, B, C])
        cond_sb = sb("cond_sb", [B, C])
        wmod_sb = sb("wmod_sb", [C, 6 * C])
        wqkv_sb = sb("wqkv_sb", [C, 3 * C])
        wproj_sb = sb("wproj_sb", [C, C])
        wqc_sb = sb("wqc_sb", [C, C])
        wkvc_sb = sb("wkvc_sb", [C, 2 * C])
        wcproj_sb = sb("wcproj_sb", [C, C])
        w1_sb = sb("w1_sb", [C, F])
        w2_sb = sb("w2_sb", [128, NF, C])
        wdh = sb("wdh", [C, 4, C])
        bmod_sb = sb("bmod_sb", [C, 6])
        bdh = sb("bdh", [C, 4])
        bv_sb = sb("bv_sb", [C, 2])
        bo_sb = sb("bo_sb", [C, 3])
        b1_sb = sb("b1_sb", [128, NF])
        bo2 = sb("bo2", [C, 2])
        ident = sb("ident", [128, 128])
        ident16 = sb("ident16", [128, 128], bf16)
        condT = sb("condT", [C, B])
        tanh_c = sb("tanh_c", [C, B])
        siluT = sb("siluT", [C, B])
        mod = sb("mod", [C, 6, B])
        gb_a = sb("gb_a", [C, B])
        gb_m = sb("gb_m", [C, B])
        eps_sb = sb("eps_sb", [128, MG])
        mhalf = sb("mhalf", [128, MG])

        qk_st = pairbuf("qk_st", [128, H, 2, GT], bf16)
        qkc_st = pairbuf("qkc_st", [128, H, 2, GT], bf16)
        v_m = pairbuf("v_m", [T, G, H, 32])
        vc_m = pairbuf("vc_m", [T, G, H, 32])
        ln = {}
        for kind, rows in (("x", T), ("ctx", S), ("x1", T)):
            ln[kind] = dict(rows=rows, stats=sb(f"{kind}_stats", [rows, G, 6]), mv=sb(f"{kind}_mv", [rows, G, 2]),
                            ve=sb(f"{kind}_ve", [rows, G]), rstd=sb(f"{kind}_rstd", [rows, G]),
                            xn=sb(f"{kind}_n", [rows, G, C]))
        xmT = sb("xmT", [C, GT])
        cT = sb("cT", [C, GS])
        x1T = sb("x1T", [C, GT])
        qkp = sb("qkp", [C, 2, 3, GT], bf16)
        qkcp = sb("qkcp", [C, 2, 3, GT], bf16)
        qkr = sb("qkr", [C, 2, GT])
        qcx = sb("qcx", [C, GT])
        kcx = sb("kcx", [C, GS])
        qcr = sb("qcr", [C, GT])
        kcr = sb("kcr", [C, GS])
        mx = sb("mx", [T, G, H])
        mxc = sb("mxc", [T, G, H])
        nm = sb("nm", [T, G, 2, H], bf16)
        nmc = sb("nmc", [T, G, 2, H], bf16)
        nmT = sb("nmT", [2 * H, G, T], bf16)
        nmcT = sb("nmcT", [2 * H, G, T], bf16)
        p_s = [sb(f"p_s{i}", [T, 4, T]) for i in range(2)]
        p_c = [sb(f"p_c{i}", [T, 4, T]) for i in range(2)]
        att = {}
        for kind in ("s", "c"):
            att[kind] = dict(sum=sb(f"{kind}_sum", [128, G, 2, T]),
                             rden=sb(f"{kind}_rden", [T, 2 * G, 8]),
                             o=sb(f"{kind}_o", [T, 2 * G, 8, D]))
        oT = sb("oT", [C, GT])
        ocT = sb("ocT", [C, GT])
        yT = sb("yT", [C, GT])
        bc3 = sb("bc3", [C, 3], bf16)
        bcr = sb("bcr", [C, 1])
        bc_rows = sb("bc_rows", [3, C], bf16)
        ones3 = sb("ones3", [3, T], bf16)

        m_stats = sb("m_stats", [T, MG, 6])
        m_mv = sb("m_mv", [T, MG, 2])
        m_ve = sb("m_ve", [T, MG])
        m_rstd = sb("m_rstd", [T, MG])
        m_n = pairbuf("m_n", [T, MG, C])
        m_nT = pairbuf("m_nT", [C, MG * T])
        hT = [t[:].rearrange("p h a t -> p (h a t)").bitcast(f32)[:, 0:NF * MG * T].rearrange(
            "p (k t) -> p k t", k=NF) for t in qk_st]
        m_y = pairbuf("m_y", [C, MG * T])
        m_out = pairbuf("m_out", [T, MG, C])

        ps = [es.enter_context(nc.psum_tensor(f"ps{i}", [128, 512], f32)) for i in range(8)]
        ps_max, ps_st, ps_o, ps_oc, ps_misc = ps[0:2], ps[2:4], ps[4], ps[5], ps[6:8]
        ps_nt, ps_h, ps_y, ps_yt = ps[4], ps[0:4], ps[5], ps[7]

        for name in ("w_in wm_in wq_in bm_in bd_in b_in x_in0 x_in1 x_in2 x_in3 c_in0 c_in1 c_in2 c_in3 z_pool z_dve zq_set zk_set zv_set zvc_set zs1_in zc0_in zc1_in "
                     "pad_set id_set wdh_set cond_t condT_set "
                     "tanh_set sig_set silu_set mod_ps mod_set bo_ps bo_set gb_set bc1_set bcr_set bc2_set bc3_set bc_ps bc_set "
                     "xt_ps qk_ps v_ps ctxt_ps kvc_ps proj_ps yt_ps x1t_ps qc_ps projc_ps mts_ps mtc_ps "
                     "smax_ps smaxc_ps st_ps stc_ps pv_ps pvc_ps ot_ps obt_ps oct_ps obct_ps "
                     "xmT_set qk0_set v_set cT_set kvc0_set y_set x1T_set qc0_set exp_set expc_set "
                     "sum_set sumc_set oT_set ocT_set "
                     "qkr_set kcr_set qcr_set mx_set mxc_set nmh_set nm_set nmch_set nmc_set nmT_set "
                     "nmcT_set rden_set o_set rdenc_set oc_set x1_set x2_set "
                     "qk1_set qk2_set kc1_set kc2_set qc1_set qc2_set "
                     "qk_in0 qk_in1 qkc_in0 qkc_in1 m_in0 m_in1 mc_in0 mc_in1 "
                     "m_stats_set m_mv_set m_ve_set m_rstd_set m_n_set m_nt_ps m_nT_set m_h_ps m_hT_set m_y_ps "
                     "m_y_set m_yt_ps m_out_set out0 out1").split():
            sem(name)
        for name in ("SP", "Pool", "DVE"):
            sem(f"held_{name}")
        for kind in ln:
            for what in ("stats", "mv", "ve", "rstd", "n"):
                sem(f"{kind}_{what}_set")

        def w(eng, name, value):
            eng.wait_ge(sems[name], value)

        def hold(eng, name, value):
            eng.wait_ge(sems[name], value)
            eng.sem_inc(sems[f"held_{eng.engine.name}"], 1)

        EMPTIED = {"proj": ("y_set", lambda p: p.n + 1), "max_c1": ("nmcT_set", lambda p: 2 * p.n + 2),
                   "y_t": ("x1_set", lambda p: p.n + 1), "ctx_t": ("cT_set", lambda p: p.n + 1),
                   "kv_c": ("kvc0_set", lambda p: p.n + 1), "x1_t": ("x1T_set", lambda p: p.n + 1),
                   "max_s0": ("nmT_set", lambda p: 2 * p.n + 1), "q_c": ("qc0_set", lambda p: p.n + 1),
                   "x_t": ("xmT_set", lambda p: p.n + 1), "qk": ("qkr_set", lambda p: p.n + 1),
                   "max_s1": ("nmT_set", lambda p: 2 * p.n + 2), "proj_c": ("x2_set", lambda p: p.n + 1),
                   "v": ("v_set", lambda p: p.n + 1),
                   "max_c0": ("nmcT_set", lambda p: 2 * p.n + 1), "o_t": ("o_set", lambda p: p.n + 1),
                   "ob_t": ("oT_set", lambda p: p.n + 1), "oc_t": ("oc_set", lambda p: p.n + 1),
                   "obc_t": ("ocT_set", lambda p: p.n + 1)}

        def batch(p, b):
            return bass.ds(2 * p.n + b, 1) if not isinstance(p.n, int) else slice(2 * p.n + b, 2 * p.n + b + 1)

        def batches(p):
            return bass.ds(2 * p.n, G) if not isinstance(p.n, int) else slice(2 * p.n, 2 * p.n + G)

        def column(tile, p, b):
            return tile[:, batch(p, b)]

        key_parts = [qkcp[:, 1, n].rearrange("c (b k) -> c b k", b=G)[:, :, 0:S] for n in range(3)]
        u32 = mybir.dt.uint32

        block = es.enter_context(nc.Block())

        @block.sync
        def _(sp):
            def o_rows(src):
                return src.rearrange("(j r m) c -> r j m c", r=2, m=2 * D)

            q4 = B // 4

            def load(n):
                sp.dma_start(xs[:, n * q4:(n + 1) * q4],
                             x[n * q4:(n + 1) * q4].rearrange("b t c -> t b c")).then_inc(sems[f"x_in{n}"], 16)
                sp.dma_start(ctx_sb[:, n * q4:(n + 1) * q4],
                             ctx[n * q4:(n + 1) * q4].rearrange("b t c -> t b c")).then_inc(sems[f"c_in{n}"], 16)

            sp.dma_start(cond_sb[:], cond).then_inc(sems["wm_in"], 16)
            sp.dma_start(wmod_sb[:], w_mod).then_inc(sems["wm_in"], 16)
            load(0)
            for dst, src in ((wqkv_sb, w_qkv), (wqc_sb, w_qc), (wkvc_sb, w_kvc)):
                sp.dma_start(dst[:], src).then_inc(sems["wq_in"], 16)
            with nc.allow_non_contiguous_dma(reason="bias columns"):
                sp.dma_start(bmod_sb[:], b_mod.rearrange("(k c) -> c k", k=6)).then_inc(sems["bm_in"], 16)
                for n, (src, at) in enumerate(((b_qkv, 0), (b_qkv, C), (b_qc, 0), (b_kvc, 0))):
                    sp.dma_start(bdh[:, n:n + 1],
                                 src[at:at + C].rearrange("(h d o) -> d h o", d=D, o=1)).then_inc(sems["bd_in"], 16)
                for n, (src, at) in enumerate(((b_qkv, 2 * C), (b_kvc, C))):
                    for r in range(2):
                        sp.dma_start(bv_sb[r * C // 2:(r + 1) * C // 2, n:n + 1],
                                     o_rows(src[at:at + C].rearrange("(c o) -> c o", o=1))[r]).then_inc(sems["b_in"], 16)
                for n, src in enumerate((b_proj, b_cproj, b_mlp2)):
                    sp.dma_start(bo_sb[:, n:n + 1], src.rearrange("(c o) -> c o", o=1)).then_inc(sems["b_in"], 16)
                sp.dma_start(b1_sb[:], b_mlp1.rearrange("(k c) -> c k", k=NF)).then_inc(sems["b_in"], 16)
            for dst, src in ((wproj_sb, w_proj), (wcproj_sb, w_cproj)):
                for r in range(2):
                    sp.dma_start(dst[r * C // 2:(r + 1) * C // 2], o_rows(src)[r]).then_inc(sems["w_in"], 16)
            sp.dma_start(w1_sb[:], w_mlp1).then_inc(sems["w_in"], 16)
            sp.dma_start(w2_sb[:], w_mlp2.rearrange("(k f) c -> f k c", k=NF)).then_inc(sems["w_in"], 16)
            for n in range(1, 4):
                load(n)

            def stack(dst, parts, name, last):
                for c, (a, b) in enumerate(COMBOS):
                    if max(a, b) == last:
                        sp.dma_start(dst[D * c:D * c + D], parts[:].rearrange("c a p t -> c (a p) t")[:, a:b + 4:b + 3 - a]
                                     ).then_inc(sems[name], 16)

            def max_rows(dst, b, src, name):
                sp.dma_start(dst[MROW:MROW + 2, :, 0, b * T:(b + 1) * T], src[:, b]).then_inc(sems[name], 16)

            def slot(s):
                a, h, f, e = (s.pair(n) for n in ("ahead", "here", "back2", "back3"))
                if f:
                    if f.first(2):
                        w(sp, f"zc{f.par}_in", 16 * 5)
                    hold(sp, "kc2_set", f.n + 1)
                    hold(sp, "qc0_set", f.n + 1)
                    if not f.first(2):
                        w(sp, "stc_ps", NU * (f.n - 1))
                    stack(qkc_st[f.par], qkcp, f"qkc_in{f.par}", 0)
                if e:
                    w(sp, "nmcT_set", 2 * e.n + 2)
                    max_rows(qkc_st[e.par], 1, nmcT, f"mc_in{e.par}")
                if f:
                    w(sp, "qc1_set", f.n + 1)
                    stack(qkc_st[f.par], qkcp, f"qkc_in{f.par}", 1)
                    w(sp, "qc2_set", f.n + 1)
                    stack(qkc_st[f.par], qkcp, f"qkc_in{f.par}", 2)
                if h:
                    w(sp, "nmT_set", 2 * h.n + 1)
                    max_rows(qk_st[h.par], 0, nmT, f"m_in{h.par}")
                if a:
                    if a.first():
                        w(sp, "zq_set", 1)
                        w(sp, "zk_set", 1)
                    if a.first(2) and a.n == 1:
                        w(sp, "zs1_in", 16 * 2)
                    hold(sp, "qk0_set", a.n + 1)
                    if not a.first(2):
                        w(sp, "st_ps", NU * (a.n - 1))
                    stack(qk_st[a.par], qkp, f"qk_in{a.par}", 0)
                if h:
                    w(sp, "nmT_set", 2 * h.n + 2)
                    max_rows(qk_st[h.par], 1, nmT, f"m_in{h.par}")
                if a:
                    w(sp, "qk1_set", a.n + 1)
                    stack(qk_st[a.par], qkp, f"qk_in{a.par}", 1)
                    w(sp, "qk2_set", a.n + 1)
                    stack(qk_st[a.par], qkp, f"qk_in{a.par}", 2)
                if a and a.first():
                    sp.dma_start(qk_st[1][ZROW:MROW], qk_st[0][ZROW:MROW]).then_inc(sems["zs1_in"], 16)
                    sp.dma_start(qk_st[1][MROW:128, :, 1], qk_st[0][MROW:128, :, 1]).then_inc(sems["zs1_in"], 16)
                    for par in range(2):
                        done = sems[f"zc{par}_in"]
                        sp.dma_start(qkc_st[par][ZROW:MROW], qk_st[0][ZROW:MROW]).then_inc(done, 16)
                        for b in range(G):
                            sp.dma_start(qkc_st[par][MROW:128, :, 1, b * T:b * T + S],
                                         qk_st[0][MROW:128, :, 1, b * T:b * T + S]).then_inc(done, 16)
                            sp.dma_start(qkc_st[par][MROW:128, :, 1, b * T + S:(b + 1) * T],
                                         qk_st[0][ZROW:ZROW + 2, :, 1, b * T + S:(b + 1) * T]).then_inc(done, 16)
                if f:
                    w(sp, "nmcT_set", 2 * f.n + 1)
                    max_rows(qkc_st[f.par], 0, nmcT, f"mc_in{f.par}")

            slots(sp, slot)

            def store(g, par):
                w(sp, "m_out_set", g + 1)
                src = m_out[par][:]
                at = bass.ds(g, 1) if not isinstance(g, int) else slice(g, g + 1)
                dst = out.rearrange("(g b) t c -> g t b c", b=MG)[at].rearrange("o t b c -> t (o b) c")
                sp.dma_start(dst, src).then_inc(sems[f"out{par}"], 16)

            with sp.Fori(0, NGRP // 2) as i:
                store(2 * i, 0)
                store(2 * i + 1, 1)
            w(sp, "out0", 16 * (NGRP // 2))
            w(sp, "out1", 16 * (NGRP // 2))

        @block.gpsimd
        def _(pool):
            nc.gpsimd.memset(ident[:], 0.0).then_inc(sems["z_pool"], 1)
            pool.wait_ge(sems["z_pool"], 1)
            nc.gpsimd.affine_select(out=ident[:], in_=ident[:], compare_op=ALU.not_equal, fill=1.0, base=0,
                                    pattern=[[-1, 128]], channel_multiplier=1).then_inc(sems["z_pool"], 1)
            pool.wait_ge(sems["z_pool"], 2)
            nc.gpsimd.tensor_copy(ident16[:], ident[:]).then_inc(sems["id_set"], 1)
            nc.gpsimd.memset(eps_sb[:], EPS).then_inc(sems["z_pool"], 1)
            nc.gpsimd.memset(mhalf[:], -0.5).then_inc(sems["z_pool"], 1)
            pool.wait_ge(sems["z_pool"], 4)
            def rstd(kind, p):
                L = ln[kind]
                w(pool, f"{kind}_mv_set", p.n + 1)
                nc.gpsimd.tensor_tensor(L["ve"][:], L["mv"][:, :, 1], eps_sb[0:L["rows"], 0:G],
                                        ALU.add).then_inc(sems[f"{kind}_ve_set"], 1)
                w(pool, f"{kind}_ve_set", p.n + 1)
                if not p.first():
                    w(pool, f"{kind}_n_set", p.n)
                nc.gpsimd.tensor_tensor(L["rstd"][:], L["ve"][:], mhalf[0:L["rows"], 0:G],
                                        ALU.pow).then_inc(sems[f"{kind}_rstd_set"], 1)

            def parts(p, rest, dst, left, mid, last, loaded):
                if not p.first():
                    q = p.shift(-1)
                    w(pool, f"{loaded}{q.par}", 16 * NCMB * (q.turn + 1))
                hold(pool, left, p.n + 1)
                nc.gpsimd.tensor_copy(dst[1], rest).then_inc(sems[mid], 1)
                w(pool, mid, p.n + 1)
                nc.gpsimd.tensor_tensor(dst[2], rest, dst[1], ALU.subtract).then_inc(sems[last], 1)

            def leave(p, whole, first, rest, ready, name):
                w(pool, ready, p.n + 1)
                nc.gpsimd.tensor_tensor(rest, whole, first, ALU.subtract).then_inc(sems[name], 1)

            def slot(s):
                far, a, h, d, f = (s.pair(n) for n in ("far", "ahead", "here", "back1", "back2"))
                if f:
                    leave(f, qcx[:], qkcp[:, 0, 0], qcr[:], "qc0_set", "qcr_set")
                    parts(f, qcr[:], [qkcp[:, 0, n] for n in range(3)], "qcr_set", "qc1_set", "qc2_set", "qkc_in")
                if a:
                    parts(a, qkr[:], [qkp[:, :, n] for n in range(3)], "qkr_set", "qk1_set", "qk2_set", "qk_in")
                if d:
                    rstd("x1", d)
                if h:
                    rstd("ctx", h)
                if d:
                    leave(d, kcx[:].rearrange("c (b k) -> c b k", b=G), key_parts[0],
                          kcr[:].rearrange("c (b k) -> c b k", b=G), "kvc0_set", "kcr_set")
                    parts(d, kcr[:].rearrange("c (b k) -> c b k", b=G), key_parts, "kcr_set", "kc1_set", "kc2_set", "qkc_in")
                if far:
                    rstd("x", far)
                    if far.first():
                        pool.wait_ge(sems["wq_in"], 16 * 3)
                        for n, (src, at) in enumerate(((wqkv_sb, 0), (wqkv_sb, C), (wqc_sb, 0), (wkvc_sb, 0))):
                            nc.gpsimd.tensor_copy(wdh[:, n].rearrange("c (d h) -> c d h", d=D),
                                                  src[:, at:at + C].rearrange("c (h d) -> c d h", d=D)).then_inc(sems["wdh_set"], 1)
                        nc.gpsimd.memset(qk_st[0][:, :, 1].bitcast(u32), 0).then_inc(sems["z_pool"], 1)
                        pool.wait_ge(sems["z_pool"], 5)
                        nc.gpsimd.memset(qk_st[0][96:128, :, 1].bitcast(u32), 0x3F803F80).then_inc(sems["zk_set"], 1)
                        hold(pool, "zk_set", 1)

            slots(pool, slot)

            def m_rstd_step(g, first=False):
                w(pool, "m_mv_set", g + 1)
                nc.gpsimd.tensor_tensor(m_ve[:], m_mv[:, :, 1], eps_sb[:, 0:MG], ALU.add).then_inc(sems["m_ve_set"], 1)
                w(pool, "m_ve_set", g + 1)
                nc.gpsimd.tensor_tensor(m_rstd[:], m_ve[:], mhalf[:, 0:MG], ALU.pow).then_inc(sems["m_rstd_set"], 1)

            with pool.Fori(0, NGRP) as g:
                m_rstd_step(g)

        @block.vector
        def _(dve):
            nc.vector.memset(qk_st[0][:, :, 0].bitcast(u32), 0).then_inc(sems["zq_set"], 1)
            dve.wait_ge(sems["cond_t"], 1)
            nc.vector.tensor_copy(condT[:], ps_max[0][:, 0:B]).then_inc(sems["condT_set"], 1)
            dve.wait_ge(sems["tanh_set"], 1)
            nc.vector.tensor_scalar(tanh_c[:], tanh_c[:], 0.5, 0.5, ALU.mult, ALU.add).then_inc(sems["sig_set"], 1)
            dve.wait_ge(sems["sig_set"], 1)
            nc.vector.tensor_tensor(siluT[:], tanh_c[:], condT[:], ALU.mult).then_inc(sems["silu_set"], 1)

            def tables():
                dve.wait_ge(sems["mod_ps"], 1)
                dve.wait_ge(sems["bm_in"], 16)
                for k in range(6):
                    last = nc.vector.tensor_scalar(mod[:, k], ps_max[0][:, k * B:(k + 1) * B], bmod_sb[:, k:k + 1],
                                                   1.0 if k in (1, 4) else 0.0, ALU.add, ALU.add)
                last.then_inc(sems["mod_set"], 1)

            def bias_tables():
                dve.wait_ge(sems["bo_ps"], 1)
                nc.vector.tensor_tensor(bo2[:], ps_max[1][:, 0:2], bo_sb[:, 0:2], ALU.add).then_inc(sems["bo_set"], 1)
                dve.wait_ge(sems["bo_set"], 1)
                dve.wait_ge(sems["mod_set"], 1)
                nc.vector.tensor_scalar(gb_a[:], mod[:, 2], bo2[:, 0:1], None, ALU.mult)
                nc.vector.tensor_scalar(gb_m[:], mod[:, 5], bo_sb[:, 2:3], None, ALU.mult).then_inc(sems["gb_set"], 1)
                nc.vector.tensor_copy(bc3[:, 0:1], bo2[:, 1:2]).then_inc(sems["bc1_set"], 1)
                dve.wait_ge(sems["bc1_set"], 1)
                nc.vector.tensor_tensor(bcr[:], bo2[:, 1:2], bc3[:, 0:1], ALU.subtract).then_inc(sems["bcr_set"], 1)
                dve.wait_ge(sems["bcr_set"], 1)
                nc.vector.tensor_copy(bc3[:, 1:2], bcr[:]).then_inc(sems["bc2_set"], 1)
                dve.wait_ge(sems["bc2_set"], 1)
                nc.vector.tensor_tensor(bc3[:, 2:3], bcr[:], bc3[:, 1:2], ALU.subtract).then_inc(sems["bc3_set"], 1)
                nc.vector.memset(ones3[:], 1.0)
                dve.wait_ge(sems["bc_ps"], 1)
                nc.vector.tensor_copy(bc_rows[:], ps_max[1][:].bitcast(bf16)[0:3, 0:C]).then_inc(sems["bc_set"], 1)

            def stats(kind, p, src):
                L = ln[kind]
                for b in range(G):
                    last = nc.vector.bn_stats(L["stats"][:, b], src(b))
                last.then_inc(sems[f"{kind}_stats_set"], 1)

            def aggregate(kind, p):
                L = ln[kind]
                hold(dve, f"{kind}_stats_set", p.n + 1)
                for b in range(G):
                    last = nc.vector.bn_aggr(L["mv"][:, b], L["stats"][:, b])
                last.then_inc(sems[f"{kind}_mv_set"], 1)

            def normalise(kind, p, src, taken):
                L = ln[kind]
                w(dve, f"{kind}_rstd_set", p.n + 1)
                if not p.first():
                    w(dve, taken, p.n)
                for b in range(G):
                    last = nc.vector.tensor_scalar(L["xn"][:, b], src(b), L["mv"][:, b, 0:1], L["rstd"][:, b:b + 1],
                                                   ALU.subtract, ALU.mult)
                last.then_inc(sems[f"{kind}_n_set"], 1)

            def arrived(name, p, rest_at):
                if p.first():
                    dve.wait_ge(sems[f"{name}0"], 16)
                elif isinstance(p.n, int) and p.n == rest_at:
                    for n in range(1, 4):
                        dve.wait_ge(sems[f"{name}{n}"], 16)

            def x_of(p):
                return lambda b: xs[:, batch(p, b)].rearrange("t o c -> t (o c)")

            def ctx_of(p):
                return lambda b: ctx_sb[:, batch(p, b)].rearrange("t o c -> t (o c)")

            def maxima(p, u, s, stream, ready, mxt, keys, done):
                b, c = divmod(u, 4)
                bank, _ = s.bank_before(MAX_RING, stream, u)
                w(dve, ready, NU * p.n + u + 1)
                src = ps_max[bank][:, :].rearrange("q (j k) -> q j k", j=4)[:, :, 0:keys]
                nc.vector.reduce_max(mxt[:, b].rearrange("q (j i) -> q j i", i=4)[:, :, c], src,
                                     AX.X).then_inc(sems[done], 1)

            def minus_max(p, b, mxt, nmt, counted, high, both, taken):
                w(dve, counted, NU * p.n + 4 * b + 4)
                if not p.first():
                    w(dve, taken, 2 * p.n + b - 1)
                nc.vector.tensor_scalar(nmt[:, b, 0], mxt[:, b], -1.0, None, ALU.mult).then_inc(sems[high], 1)
                w(dve, high, 2 * p.n + b + 1)
                nc.vector.scalar_tensor_tensor(nmt[:, b, 1], mxt[:, b], -1.0, nmt[:, b, 0], ALU.mult,
                                               ALU.subtract).then_inc(sems[both], 1)

            def attention_out(p, kind, job, ready, rden_name, name, taken):
                src = ps_misc[BANK[job]][:].rearrange("q (r m x) -> q r m x", r=2 * G, x=2 * D)
                w(dve, ready, p.n + 1)
                nc.vector.reciprocal(att[kind]["rden"][:], src[:, :, :, D]).then_inc(sems[rden_name], 1)
                if not p.first():
                    w(dve, taken, p.n)
                w(dve, rden_name, p.n + 1)
                nc.vector.tensor_tensor(att[kind]["o"][:], src[:, :, :, 0:D],
                                        att[kind]["rden"][:].unsqueeze(3).to_broadcast([T, 2 * G, 8, D]),
                                        ALU.mult).then_inc(sems[name], 1)

            def rest(psum, bias, part, dst):
                return nc.vector.scalar_tensor_tensor(dst, psum, bias, part, ALU.add, ALU.subtract)

            def residual(p, ready, job, name):
                w(dve, ready, p.n + 1)
                nc.vector.tensor_tensor(xs[:, batches(p)], xs[:, batches(p)],
                                        ps_misc[BANK[job]][:, 0:GT].rearrange("t (b c) -> t b c", b=G),
                                        ALU.add).then_inc(sems[name], 1)

            def around(tiles, keys, n, done):
                for vt in tiles:
                    last = nc.vector.memset(vt[:], 0.0)
                last.then_inc(sems["z_dve"], 1)
                dve.wait_ge(sems["z_dve"], n)
                for vt in tiles:
                    for s_ in range(2):
                        last = nc.vector.memset(vt[0:keys].rearrange("t b (m s) n -> t (b m) s n", s=2)[
                            :, :, s_, 2 * D * s_ + D:2 * D * s_ + D + 1], 1.0)
                last.then_inc(sems[done], 1)

            def group(g):
                return bass.ds(MG * g, MG) if not isinstance(g, int) else slice(MG * g, MG * g + MG)

            def one(g, b):
                at = bass.ds(MG * g + b, 1) if not isinstance(g, int) else slice(MG * g + b, MG * g + b + 1)
                return xs[:, at].rearrange("t o c -> t (o c)")

            def m_norm(g, par, first=False):
                if not first:
                    hold(dve, "m_n_set", g)
                for b in range(MG):
                    last = nc.vector.bn_stats(m_stats[:, b], one(g, b))
                last.then_inc(sems["m_stats_set"], 1)
                hold(dve, "m_stats_set", g + 1)
                for b in range(MG):
                    last = nc.vector.bn_aggr(m_mv[:, b], m_stats[:, b])
                last.then_inc(sems["m_mv_set"], 1)
                if not first and not (isinstance(g, int) and g < 2):
                    hold(dve, "m_nt_ps", g - 1)
                w(dve, "m_rstd_set", g + 1)
                for b in range(MG):
                    last = nc.vector.tensor_scalar(m_n[par][:, b], one(g, b), m_mv[:, b, 0:1], m_rstd[:, b:b + 1],
                                                   ALU.subtract, ALU.mult)
                last.then_inc(sems["m_n_set"], 1)

            def m_residual(g, par, first=False):
                w(dve, "m_yt_ps", g + 1)
                if not first:
                    w(dve, f"out{par}", 16 * (g // 2) if isinstance(g, int) else 8 * (g - par))
                nc.vector.tensor_tensor(m_out[par][:], xs[:, group(g)],
                                        ps_yt[:, :].rearrange("t (b c) -> t b c", b=MG), ALU.add).then_inc(sems["m_out_set"], 1)

            def slot(s):
                far, a, h, d, f, e = (s.pair(n) for n in ("far", "ahead", "here", "back1", "back2", "back3"))
                for t in range(TICKS):
                    if t == 6 and s.last(1):
                        dve.wait_ge(sems["x2_set"], NPAIR - 2)
                        m_norm(0, 0, True)
                    if t == 0 and s.last():
                        m_norm(1, 1)
                    if t == 9 and d:
                        residual(d, "yt_ps", "y_t", "x1_set")
                    if t == 10 and e:
                        attention_out(e, "c", "oc_t", "oct_ps", "rdenc_set", "oc_set", "obct_ps")
                    if t == 12 and d:
                        normalise("x1", d, x_of(d), "x1t_ps")

                    use = s.unit(self_max(t))
                    if use:
                        maxima(*use, s, "self", "smax_ps", mx, T, "mx_set")
                    use = s.unit(cross_max(t))
                    if use:
                        maxima(*use, s, "cross", "smaxc_ps", mxc, S, "mxc_set")

                    if t == 3 and h:
                        minus_max(h, 0, mx, nm, "mx_set", "nmh_set", "nm_set", "mts_ps")
                    if t == 7 and h:
                        minus_max(h, 1, mx, nm, "mx_set", "nmh_set", "nm_set", "mts_ps")
                    if t == 11 and f:
                        minus_max(f, 0, mxc, nmc, "mxc_set", "nmch_set", "nmc_set", "mtc_ps")
                    if t == 15 and f:
                        minus_max(f, 1, mxc, nmc, "mxc_set", "nmch_set", "nmc_set", "mtc_ps")
                    if t == 0 and a:
                        normalise("x", a, x_of(a), "xt_ps")
                        if a.first():
                            tables()
                    if t == 2 and d:
                        attention_out(d, "s", "o_t", "ot_ps", "rden_set", "o_set", "obt_ps")
                    if t == 6 and a:
                        w(dve, "qk0_set", a.n + 1)
                        if not a.first():
                            w(dve, "qk2_set", a.n)
                        rest(ps_misc[BANK["qk"]][:, 0:GT], bdh[:, 0:1], qkp[:, 0, 0], qkr[:, 0])
                        rest(ps_misc[BANK["qk"]][:, GT:2 * GT], bdh[:, 1:2], qkp[:, 1, 0],
                             qkr[:, 1]).then_inc(sems["qkr_set"], 1)
                    if t == 9 and d:
                        hold(dve, "x1_set", d.n + 1)
                        stats("x1", d, x_of(d))
                        aggregate("x1", d)
                    if t == 10 and h:
                        arrived("c_in", h, 2 * LOOP[0] - 1)
                        stats("ctx", h, ctx_of(h))
                        aggregate("ctx", h)
                    if t == 12:
                        if far:
                            arrived("x_in", far, 2 * LOOP[0])
                            stats("x", far, x_of(far))
                            aggregate("x", far)
                            if far.first():
                                around(v_m, T, 1, "zv_set")
                    if t == 14:
                        if e:
                            residual(e, "projc_ps", "proj_c", "x2_set")
                    if t == 15:
                        if h:
                            normalise("ctx", h, ctx_of(h), "ctxt_ps")
                if a and a.first():
                    bias_tables()
                    nc.vector.memset(qkcp[:].bitcast(u32), 0).then_inc(sems["pad_set"], 1)
                    around(vc_m, S, 2, "zvc_set")

            slots(dve, slot)

            dve.wait_ge(sems["x2_set"], NPAIR)
            m_norm(2, 0)
            m_residual(0, 0, True)
            m_norm(3, 1)
            m_residual(1, 1, True)
            with dve.Fori(1, NGRP // 2 - 1) as i:
                m_norm(2 * i + 2, 0)
                m_residual(2 * i, 0)
                m_norm(2 * i + 3, 1)
                m_residual(2 * i + 1, 1)
            m_residual(NGRP - 2, 0)
            m_residual(NGRP - 1, 1)

        @block.scalar
        def _(act):
            act.wait_ge(sems["condT_set"], 1)
            nc.scalar.activation(tanh_c[:], condT[:], ACT.Tanh, scale=0.5).then_inc(sems["tanh_set"], 1)

            def exps(p, u, s, stream, ready, dst, name, pv):
                bank, _ = s.bank_before(EXP_RING, stream, u)
                w(act, ready, NU * p.n + u + 1)
                if u >= 2 or not p.first():
                    w(act, pv, NU * p.n + u - 1)
                nc.scalar.activation(dst[u % 2][:].rearrange("k j q -> k (j q)"), ps_st[bank][:, :],
                                     ACT.Exp, scale=SCALE).then_inc(sems[name], 1)

            def values(dst, keys, src):
                for s_ in range(2):
                    for b in range(G):
                        last = nc.scalar.activation(
                            dst[0:keys, b].rearrange("t (m s) n -> t m s n", s=2)[:, :, s_, 2 * D * s_:2 * D * s_ + D],
                            src[:, b * C:(b + 1) * C].rearrange("t (m s d) -> t m s d", s=2, d=D)[:, :, s_, :], ACT.Copy)
                return last

            def empty_max(p, b, job, ready, dst, name, loaded):
                w(act, ready, 2 * p.n + b + 1)
                if not p.first():
                    q = p.shift(-1)
                    w(act, f"{loaded}{q.par}", 16 * G * (q.turn + 1))
                nc.scalar.activation(dst[:, b], ps_misc[BANK[job]][:].bitcast(bf16)[0:2 * H, 0:T],
                                     ACT.Copy).then_inc(sems[name], 1)

            def sums(p, kind, src, ready, name, taken):
                w(act, ready, NU * p.n + NU)
                if not p.first():
                    w(act, taken, p.n)
                nc.scalar.activation(att[kind]["sum"][:].rearrange("c b r q -> c (b r q)"), src[:, :],
                                     ACT.Copy).then_inc(sems[name], 1)

            def copy(dst, src, ready, p, name, taken):
                w(act, ready, p.n + 1)
                if not p.first():
                    w(act, taken, p.n)
                nc.scalar.activation(dst, src, ACT.Copy).then_inc(sems[name], 1)

            def one(tile, g, b):
                return tile[:, bass.ds(MG * g + b, 1) if not isinstance(g, int) else slice(MG * g + b, MG * g + b + 1)]

            def m_modulate(g, par, first=False):
                w(act, "m_nt_ps", g + 1)
                for b in range(MG):
                    last = nc.scalar.activation(m_nT[par][:, b * T:(b + 1) * T], ps_nt[:, b * T:(b + 1) * T], ACT.Identity,
                                                bias=one(mod[:, 3], g, b), scale=one(mod[:, 4], g, b))
                last.then_inc(sems["m_nT_set"], 1)

            def m_gelu(g, par, chunks=range(NF)):
                for k in chunks:
                    w(act, "m_h_ps", NF * g + k + 1)
                    nc.scalar.activation(hT[par][:, k], ps_h[k][:, :], ACT.Gelu_apprx_tanh,
                                         bias=b1_sb[:, k:k + 1]).then_inc(sems["m_hT_set"], 1)

            def m_gate(g, par, first=False):
                w(act, "m_y_ps", g + 1)
                for b in range(MG):
                    last = nc.scalar.activation(m_y[par][:, b * T:(b + 1) * T], ps_y[:, b * T:(b + 1) * T], ACT.Identity,
                                                bias=one(gb_m, g, b), scale=one(mod[:, 5], g, b))
                last.then_inc(sems["m_y_set"], 1)

            def slot(s):
                a, h, d, f, e = (s.pair(n) for n in ("ahead", "here", "back1", "back2", "back3"))
                for t in range(TICKS):
                    if t == 10 and s.last(1):
                        m_modulate(0, 0, True)
                    if t == 9 and s.last():
                        m_modulate(1, 1)
                    if t == 1 and e:
                        empty_max(e, 1, "max_c1", "mtc_ps", nmcT, "nmcT_set", "mc_in")
                    if t == 9 and h:
                        empty_max(h, 1, "max_s1", "mts_ps", nmT, "nmT_set", "m_in")
                    if t == 13 and f:
                        empty_max(f, 0, "max_c0", "mtc_ps", nmcT, "nmcT_set", "mc_in")
                    if t == 1 and d:
                        sums(d, "s", ps_o, "pv_ps", "sum_set", "ot_ps")
                    if t == 3 and d:
                        copy(cT[:], ps_misc[BANK["ctx_t"]][:, 0:GS], "ctxt_ps", d, "cT_set", "kvc_ps")
                    if t == 4 and a:
                        w(act, "xt_ps", a.n + 1)
                        if a.first():
                            act.wait_ge(sems["mod_set"], 1)
                        else:
                            w(act, "v_ps", a.n)
                        for b in range(G):
                            last = nc.scalar.activation(xmT[:, b * T:(b + 1) * T],
                                                        ps_misc[BANK["x_t"]][:, b * T:(b + 1) * T], ACT.Identity,
                                                        bias=column(mod[:, 0], a, b), scale=column(mod[:, 1], a, b))
                        last.then_inc(sems["xmT_set"], 1)
                    if t == 5 and d:
                        copy(oT[:], ps_misc[BANK["ob_t"]][:, 0:GT], "obt_ps", d, "oT_set", "proj_ps")
                    if t == 6 and a:
                        w(act, "qk_ps", a.n + 1)
                        src = ps_misc[BANK["qk"]]
                        if a.first():
                            act.wait_ge(sems["bd_in"], 16 * 4)
                        else:
                            q = a.shift(-1)
                            w(act, f"qk_in{q.par}", 16 * NCMB * (q.turn + 1))
                        nc.scalar.activation(qkp[:, 0, 0], src[:, 0:GT], ACT.Identity, bias=bdh[:, 0:1])
                        nc.scalar.activation(qkp[:, 1, 0], src[:, GT:2 * GT], ACT.Identity,
                                             bias=bdh[:, 1:2]).then_inc(sems["qk0_set"], 1)
                    if t == 7 and d:
                        w(act, "proj_ps", d.n + 1)
                        if not d.first():
                            w(act, "yt_ps", d.n)
                        for b in range(G):
                            last = nc.scalar.activation(yT[:, b * T:(b + 1) * T],
                                                        ps_misc[BANK["proj"]][:, b * T:(b + 1) * T], ACT.Identity,
                                                        bias=column(gb_a, d, b), scale=column(mod[:, 2], d, b))
                        last.then_inc(sems["y_set"], 1)
                    if t == 8 and a:
                        w(act, "v_ps", a.n + 1)
                        if a.first():
                            act.wait_ge(sems["zv_set"], 1)
                        if not a.first(2):
                            w(act, "pv_ps", NU * (a.n - 1))
                        values(v_m[a.par], T, ps_misc[BANK["v"]][:, 0:G * C]).then_inc(sems["v_set"], 1)
                    if t == 9 and e:
                        sums(e, "c", ps_oc, "pvc_ps", "sumc_set", "oct_ps")
                    if t == 11 and d:
                        w(act, "kvc_ps", d.n + 1)
                        src = ps_misc[BANK["kv_c"]]
                        if d.first():
                            act.wait_ge(sems["pad_set"], 1)
                            act.wait_ge(sems["zvc_set"], 1)
                        else:
                            q = d.shift(-1)
                            w(act, f"qkc_in{q.par}", 16 * NCMB * (q.turn + 1))
                            w(act, "kcr_set", d.n)
                        nc.scalar.activation(key_parts[0], src[:, 0:GS].rearrange("c (b k) -> c b k", b=G), ACT.Identity,
                                             bias=bdh[:, 3:4])
                        nc.scalar.activation(kcx[:], src[:, 0:GS], ACT.Identity, bias=bdh[:, 3:4])
                        if not d.first(2):
                            w(act, "pvc_ps", NU * (d.n - 1))
                        values(vc_m[d.par], S, src[0:S, GS:GS + G * C]).then_inc(sems["kvc0_set"], 1)
                    if t == 10 and s.last():
                        m_gelu(0, 0, range(0, 2))
                    if t == 12 and e:
                        copy(ocT[:], ps_misc[BANK["obc_t"]][:, 0:GT], "obct_ps", e, "ocT_set", "projc_ps")
                    if t == 14 and d:
                        w(act, "x1t_ps", d.n + 1)
                        nc.scalar.activation(x1T[:], ps_misc[BANK["x1_t"]][:, 0:GT], ACT.Copy).then_inc(sems["x1T_set"], 1)
                    if t == 15 and d:
                        w(act, "qc_ps", d.n + 1)
                        if not d.first():
                            q = d.shift(-1)
                            w(act, f"qkc_in{q.par}", 16 * NCMB * (q.turn + 1))
                            w(act, "qcr_set", d.n)
                        nc.scalar.activation(qkcp[:, 0, 0], ps_misc[BANK["q_c"]][:, 0:GT], ACT.Identity, bias=bdh[:, 2:3])
                        nc.scalar.activation(qcx[:], ps_misc[BANK["q_c"]][:, 0:GT], ACT.Identity,
                                             bias=bdh[:, 2:3]).then_inc(sems["qc0_set"], 1)
                    use = s.unit(self_exp(t))
                    if use:
                        exps(*use, s, "self", "st_ps", p_s, "exp_set", "pv_ps")
                    use = s.unit(cross_exp(t))
                    if use:
                        exps(*use, s, "cross", "stc_ps", p_c, "expc_set", "pvc_ps")
                    if t == 5 and h:
                        empty_max(h, 0, "max_s0", "mts_ps", nmT, "nmT_set", "m_in")

                if s.last():
                    m_gelu(0, 0, range(2, NF))

            slots(act, slot)

            m_gate(0, 0)
            m_gelu(1, 1)
            m_modulate(2, 0)
            m_gate(1, 1)
            with act.Fori(1, NGRP // 2 - 1) as i:
                for k in range(2):
                    m_gelu(2 * i + k, k)
                    m_modulate(2 * i + k + 1, (k + 1) % 2)
                    m_gate(2 * i + k, k)
            m_gelu(NGRP - 2, 0)
            m_modulate(NGRP - 1, 1)
            m_gate(NGRP - 2, 0)
            m_gelu(NGRP - 1, 1)
            m_gate(NGRP - 1, 1)

        @block.tensor
        def _(pe):
            mm, tr = nc.tensor.matmul, nc.tensor.transpose

            pe.wait_ge(sems["id_set"], 1)
            pe.wait_ge(sems["wm_in"], 16 * 2)
            tr(ps_max[0][:, 0:B], cond_sb[:], ident[0:B, 0:B]).then_inc(sems["cond_t"], 1)
            pe.wait_ge(sems["silu_set"], 1)
            for k in range(6):
                last = mm(ps_max[0][:, k * B:(k + 1) * B], wmod_sb[:, k * C:(k + 1) * C], siluT[:], start=True, stop=True)
            last.then_inc(sems["mod_ps"], 1)

            def bank(s, name):
                before = s.job_before(name)
                if before:
                    job, p = before
                    name_, count = EMPTIED[job]
                    w(pe, name_, count(p))
                return ps_misc[BANK[name]]

            def scores(p, u, dst, st, keys, counted):
                b, c = divmod(u, 4)
                for j in range(4):
                    h = 4 * j + c
                    last = mm(dst[:, j * T:j * T + keys], st[p.par][0:MROW, h, 0, b * T:(b + 1) * T],
                              st[p.par][0:MROW, h, 1, b * T:b * T + keys], start=True, stop=True)
                last.then_inc(sems[counted], 1)

            def scores_t(p, u, dst, st, counted):
                b, c = divmod(u, 4)
                for j in range(4):
                    h = 4 * j + c
                    last = mm(dst[:, j * T:(j + 1) * T], st[p.par][:, h, 1, b * T:(b + 1) * T],
                              st[p.par][:, h, 0, b * T:(b + 1) * T], start=True, stop=True)
                last.then_inc(sems[counted], 1)

            def values(p, u, probs, dst, vt, counted):
                b, c = divmod(u, 4)
                r, s_ = divmod(c, 2)
                at = (b * 2 + r) * T
                for j in range(4):
                    last = mm(dst[32 * j:32 * j + 32, at:at + T], vt[p.par][:, b, 4 * j + c], probs[u % 2][:, j],
                              start=(s_ == 0), stop=(s_ == 1))
                last.then_inc(sems[counted], 1)

            def ring_bank(s, uses, tiles, stream, u, names):
                n, before = s.bank_before(uses, stream, u)
                if before:
                    name, q, unit = before
                    w(pe, names[name], NU * q.n + unit + 1)
                return tiles[n]

            def m_transpose(g, par, first=False):
                w(pe, "m_n_set", g + 1)
                if not first:
                    w(pe, "m_nT_set", g)
                for b in range(MG):
                    last = tr(ps_nt[:, b * T:(b + 1) * T], m_n[par][:, b], ident[:])
                last.then_inc(sems["m_nt_ps"], 1)

            def m_up(g, par, first=False, chunks=range(NF)):
                w(pe, "m_nT_set", g + 1)
                for k in chunks:
                    if not first:
                        w(pe, "m_hT_set", NF * g - NF + k + 1)
                    mm(ps_h[k][:, :], w1_sb[:, k * 128:(k + 1) * 128], m_nT[par][:], start=True,
                       stop=True).then_inc(sems["m_h_ps"], 1)

            def m_down(g, par, first=False):
                if not first:
                    w(pe, "m_y_set", g)
                for k in range(NF):
                    w(pe, "m_hT_set", NF * g + k + 1)
                    last = mm(ps_y[:, :], w2_sb[:, k], hT[par][:, k], start=(k == 0), stop=(k == NF - 1))
                last.then_inc(sems["m_y_ps"], 1)

            def m_back(g, par, first=False):
                w(pe, "m_y_set", g + 1)
                if not first:
                    w(pe, "m_out_set", g)
                for b in range(MG):
                    last = tr(ps_yt[:, b * C:(b + 1) * C], m_y[par][:, b * T:(b + 1) * T], ident[:])
                last.then_inc(sems["m_yt_ps"], 1)

            def slot(s):
                a, h, d, f, e = (s.pair(n) for n in ("ahead", "here", "back1", "back2", "back3"))
                max_read = {"self": "mx_set", "cross": "mxc_set"}
                exp_read = {"self": "exp_set", "cross": "expc_set"}

                def transposed(job, kind, p, rows, counted):
                    dst = bank(s, job)
                    w(pe, f"{kind}_n_set", p.n + 1)
                    for b in range(G):
                        last = tr(dst[:, b * rows:(b + 1) * rows], ln[kind]["xn"][:, b], ident[0:rows, 0:rows])
                    last.then_inc(sems[counted], 1)

                def flip(job, p, srcs, ready, counted):
                    dst = bank(s, job)
                    w(pe, ready, p.n + 1)
                    for n, src in enumerate(srcs):
                        last = tr(dst[:, n * 128:(n + 1) * 128], src, ident[:])
                    last.then_inc(sems[counted], 1)

                def flip_sums(job, kind, p, ready, counted):
                    flip(job, p, [att[kind]["sum"][:, b, r] for b in range(G) for r in range(2)], ready, counted)

                def flip_out(job, kind, p, ready, counted):
                    flip(job, p, [att[kind]["o"][:, 2 * b:2 * b + 2].rearrange("q r m d -> q (r m d)") for b in range(G)],
                         ready, counted)

                def flip_y(job, src, p, ready, counted):
                    flip(job, p, [src[:, b * T:(b + 1) * T] for b in range(G)], ready, counted)

                def project(job, p, weights, src, ready, counted, cols=GT):
                    dst = bank(s, job)
                    w(pe, ready, p.n + 1)
                    mm(dst[:, 0:cols], weights, src, start=True, stop=True).then_inc(sems[counted], 1)

                def max_t(job, p, b, src, ready, counted):
                    dst = bank(s, job)
                    w(pe, ready, 2 * p.n + b + 1)
                    tr(dst[:].bitcast(bf16)[0:2 * H, 0:T], src[:, b].rearrange("q r h -> q (r h)"),
                       ident16[:]).then_inc(sems[counted], 1)

                for t in range(TICKS):
                    use = s.unit(self_max(t))
                    if use:
                        p, u = use
                        dst = ring_bank(s, MAX_RING, ps_max, "self", u, max_read)
                        if u == 0:
                            w(pe, f"qk_in{p.par}", 16 * NCMB * (p.turn + 1))
                        scores(p, u, dst, qk_st, T, "smax_ps")
                    use = s.unit(cross_max(t))
                    if use:
                        p, u = use
                        dst = ring_bank(s, MAX_RING, ps_max, "cross", u, max_read)
                        if u == 0:
                            w(pe, f"qkc_in{p.par}", 16 * NCMB * (p.turn + 1))
                        scores(p, u, dst, qkc_st, S, "smaxc_ps")
                    use = s.unit(self_exp(t))
                    if use:
                        p, u = use
                        dst = ring_bank(s, EXP_RING, ps_st, "self", u, exp_read)
                        if u % 4 == 0:
                            w(pe, f"m_in{p.par}", 16 * (G * p.turn + u // 4 + 1))
                        scores_t(p, u, dst, qk_st, "st_ps")
                    use = s.unit(cross_exp(t))
                    if use:
                        p, u = use
                        dst = ring_bank(s, EXP_RING, ps_st, "cross", u, exp_read)
                        if u % 4 == 0:
                            w(pe, f"mc_in{p.par}", 16 * (G * p.turn + u // 4 + 1))
                        scores_t(p, u, dst, qkc_st, "stc_ps")
                    if t == 2 and d:
                        flip_sums("o_t", "s", d, "sum_set", "ot_ps")
                    if t == 10 and e:
                        flip_sums("oc_t", "c", e, "sumc_set", "oct_ps")
                    if t == 5 and h:
                        max_t("max_s0", h, 0, nm, "nm_set", "mts_ps")
                    use = s.unit(self_pv(t))
                    if use:
                        p, u = use
                        w(pe, "exp_set", NU * p.n + u + 1)
                        if u == 0:
                            w(pe, "v_set", p.n + 1)
                            if not p.first():
                                w(pe, "sum_set", p.n)
                        values(p, u, p_s, ps_o, v_m, "pv_ps")
                    use = s.unit(cross_pv(t))
                    if use:
                        p, u = use
                        w(pe, "expc_set", NU * p.n + u + 1)
                        if u == 0 and not p.first():
                            w(pe, "sumc_set", p.n)
                        values(p, u, p_c, ps_oc, vc_m, "pvc_ps")

                    if s.last(1) and t == 7:
                        pe.wait_ge(sems["sum_set"], NPAIR)
                        m_transpose(0, 0, True)
                    if s.last():
                        if t in (1, 3):
                            pe.wait_ge(sems["mxc_set"], NU * NPAIR)
                            m_up(0, 0, True, (t // 2,))
                        if t == 5:
                            m_transpose(1, 1)
                        if t in (8, 10):
                            pe.wait_ge(sems["expc_set"], NU * NPAIR)
                            m_up(0, 0, True, (t // 2 - 2,))
                        if t == 12:
                            m_up(1, 1, chunks=range(0, 2))
                    if t == 0 and e:
                        max_t("max_c1", e, 1, nmc, "nmc_set", "mtc_ps")
                    if t == 2 and d:
                        transposed("ctx_t", "ctx", d, S, "ctxt_ps")
                    if t == 3 and a:
                        transposed("x_t", "x", a, T, "xt_ps")
                    if t == 4:
                        if d:
                            flip_out("ob_t", "s", d, "o_set", "obt_ps")
                    if t == 5 and a:
                        dst = bank(s, "qk")
                        if a.first():
                            pe.wait_ge(sems["wdh_set"], 4)
                        w(pe, "xmT_set", a.n + 1)
                        mm(dst[:, 0:GT], wdh[:, 0], xmT[:], start=True, stop=True)
                        mm(dst[:, GT:2 * GT], wdh[:, 1], xmT[:], start=True, stop=True).then_inc(sems["qk_ps"], 1)
                    if t == 6 and d:
                        project("proj", d, wproj_sb[:], oT[:], "oT_set", "proj_ps")
                    if t == 7 and a:
                        dst = bank(s, "v")
                        for b in range(G):
                            last = mm(dst[:, b * C:(b + 1) * C], xmT[:, b * T:(b + 1) * T], wqkv_sb[:, 2 * C:3 * C],
                                      start=True, stop=True)
                        last.then_inc(sems["v_ps"], 1)
                    if t == 8:
                        if d:
                            flip_y("y_t", yT, d, "y_set", "yt_ps")
                        if h:
                            max_t("max_s1", h, 1, nm, "nm_set", "mts_ps")
                    if t == 10 and d:
                        dst = bank(s, "kv_c")
                        w(pe, "cT_set", d.n + 1)
                        mm(dst[:, 0:GS], wdh[:, 3], cT[:], start=True, stop=True)
                        for b in range(G):
                            last = mm(dst[0:S, GS + b * C:GS + (b + 1) * C], cT[:, b * S:(b + 1) * S],
                                      wkvc_sb[:, C:2 * C], start=True, stop=True)
                        last.then_inc(sems["kvc_ps"], 1)
                    if t == 11 and e:
                        flip_out("obc_t", "c", e, "oc_set", "obct_ps")
                    if t == 12 and f:
                        max_t("max_c0", f, 0, nmc, "nmc_set", "mtc_ps")
                    if t == 13 and d:
                        transposed("x1_t", "x1", d, T, "x1t_ps")
                    if t == 13 and e:
                        dst = bank(s, "proj_c")
                        w(pe, "ocT_set", e.n + 1)
                        mm(dst[:, 0:G * C], ones3[:], bc_rows[:].unsqueeze(1).to_broadcast([3, G, C]), start=True, stop=False)
                        for b in range(G):
                            last = mm(dst[:, b * C:(b + 1) * C], ocT[:, b * T:(b + 1) * T], wcproj_sb[:], start=False,
                                      stop=(b == G - 1))
                        last.then_inc(sems["projc_ps"], 1)
                    if t == 14 and d:
                        project("q_c", d, wdh[:, 2], x1T[:], "x1T_set", "qc_ps")
                if a and a.first():
                    pe.wait_ge(sems["w_in"], 16 * 6)
                    pe.wait_ge(sems["b_in"], 16 * 8)
                    mm(ps_max[1][:, 0:1], wproj_sb[:], bv_sb[:, 0:1], start=True, stop=True)
                    mm(ps_max[1][:, 1:2], wcproj_sb[:], bv_sb[:, 1:2], start=True, stop=True).then_inc(sems["bo_ps"], 1)
                    pe.wait_ge(sems["bc3_set"], 1)
                    tr(ps_max[1][:].bitcast(bf16)[0:3, 0:C], bc3[:], ident16[:]).then_inc(sems["bc_ps"], 1)
                    pe.wait_ge(sems["bc_set"], 1)

            slots(pe, slot)

            pe.wait_ge(sems["sumc_set"], NPAIR)
            m_down(0, 0, True)
            m_up(1, 1, chunks=range(2, NF))
            pe.wait_ge(sems["x2_set"], NPAIR)
            m_back(0, 0, True)
            m_transpose(2, 0)
            m_down(1, 1)
            with pe.Fori(1, NGRP // 2 - 1) as i:
                for k in range(2):
                    m_up(2 * i + k, k)
                    m_back(2 * i + k - 1, (k + 1) % 2)
                    m_transpose(2 * i + k + 1, (k + 1) % 2)
                    m_down(2 * i + k, k)
            m_up(NGRP - 2, 0)
            m_back(NGRP - 3, 1)
            m_transpose(NGRP - 1, 1)
            m_down(NGRP - 2, 0)
            m_up(NGRP - 1, 1)
            m_back(NGRP - 2, 0)
            m_down(NGRP - 1, 1)
            m_back(NGRP - 1, 1)


_INS = ["x", "cond_1024", "ctx_1024"] + ["L0_xcond_" + n for n in (
    "W_mod", "b_mod", "W_qkv", "b_qkv", "W_proj", "b_proj", "W_qc", "b_qc", "W_kvc", "b_kvc", "W_cproj", "b_cproj",
    "W_mlp1", "b_mlp1", "W_mlp2", "b_mlp2")]


def kernel(**inputs):
    import numpy as np
    import concourse.bacc as bacc
    from concourse.bass_utils import run_bass_kernel_spmd

    nc = bacc.Bacc("TRN2", target_bir_lowering=False, num_devices=1)
    arrays, args = {}, []
    for name in _INS:
        a = np.ascontiguousarray(inputs[name])
        arrays[name] = a
        args.append(nc.dram_tensor(name, a.shape, mybir.dt.from_np(a.dtype), kind="ExternalInput").ap())
    args.append(nc.dram_tensor("out", (B, T, C), mybir.dt.float32, kind="ExternalOutput").ap())
    block_kernel(nc, *args)
    r = run_bass_kernel_spmd(nc, [arrays], core_ids=[0])
    return r.results[0]["out"]
```
